# Optimizing a Trainium2 kernel written in Bass

```python
import numpy as np
import jax
import jax.numpy as jnp

def _softmax(x, axis=-1):
    return jax.nn.softmax(x, axis=axis)

def _gelu(x):
    return jax.nn.gelu(x, approximate=True)

def _silu(x):
    return jax.nn.silu(x)

def _sigmoid(x):
    return jax.nn.sigmoid(x)

def _layernorm(x, axis=-1, eps=1e-05):
    m = jnp.mean(x, axis=axis, keepdims=True)
    v = jnp.var(x, axis=axis, keepdims=True)
    return (x - m) / jnp.sqrt(v + eps)

def _scatter_add(tgt, idx, src, axis=0):
    return tgt.at[idx].add(src)

def _segment_sum(src, seg, n):
    return jax.ops.segment_sum(src, seg, n)
kernel_name = 'mk_flamingo_gated_d1_seqx_r4_4b00b1'

def setup_inputs(seed: int=0):
    np.random.seed(seed)
    _w = jnp.asarray

    def _rec_inputs():
        import jax
        import jax.numpy as jnp
        _rk = jax.random.key(seed)
        x = -0.0002928 + 1 * jax.random.normal(jax.random.fold_in(_rk, 1), (8, 256, 512), jnp.float32)
        _lenS = 256 - jax.random.randint(jax.random.fold_in(_rk, 7), (8,), 0, max(1, 256 // 4) + 1, jnp.int32)
        _lenS2 = 256 - jax.random.randint(jax.random.fold_in(_rk, 8), (8,), 0, max(1, 256 // 4) + 1, jnp.int32)
        fside_S2_0 = -0.00337071 + 1.01897 * jax.random.normal(jax.random.fold_in(_rk, 11), (256,), jnp.float32)
        _ctx_2048P = jax.random.normal(jax.random.fold_in(_rk, 12), (8, 16, 512), jnp.float32)
        _ctx_2048c = jax.random.dirichlet(jax.random.fold_in(_rk, 512), 0.3 * jnp.ones((16,), jnp.float32), (8, 256))
        _ctx_2048t = jnp.einsum('bsk,bkd->bsd', _ctx_2048c, _ctx_2048P)
        _ctx_2048t = _ctx_2048t * jax.lax.rsqrt(jnp.mean(jnp.square(_ctx_2048t)) + 1e-12) * 0.953939
        ctx_2048 = 0.000675642 + 1.00031 * (_ctx_2048t + 0.3 * jax.random.normal(jax.random.fold_in(_rk, 612), (8, 256, 512), jnp.float32))
        _g = jax.random.normal(jax.random.fold_in(_rk, 9001), (2, 1), jnp.float32)
        _g = jnp.sign(_g) * jnp.maximum(jnp.abs(_g), 1.0) + (_g == 0) * 1.0
        g_xattn = _g[0]
        g_ffn = _g[1]
        return (x, fside_S2_0, ctx_2048, g_xattn, g_ffn)
    x, fside_S2_0, ctx_2048, g_xattn, g_ffn = _rec_inputs()

    def _L0_xattn_setup():
        import jax, jax.numpy as jnp
        import numpy as np
        key = jax.random.key(seed)
        ks = jax.random.split(key, 5)
        B, D, L, NH = (2, 256, 512, 8)
        H = D // NH
        return {'v': jax.random.normal(ks[0], (B, D, L), jnp.float32), 'k': jax.random.normal(ks[1], (H, L), jnp.float32) * 0.1, 'bias': jax.random.normal(ks[2], (D,), jnp.float32), 'x1': jax.random.normal(ks[3], (B, D, L), jnp.float32), 'x2': jax.random.normal(ks[4], (B, D, L), jnp.float32), 'num_heads': NH}
    _L0_xattn_all = _L0_xattn_setup()
    _L0_xattn_in = {k: v for k, v in _L0_xattn_all.items() if k in ('k',)}
    del _L0_xattn_all

    def _L0_ffn_setup():
        import jax, jax.numpy as jnp
        import numpy as np
        SEQ, BS, H, I, E = (512, 4, 512, 1024, 8)
        key = jax.random.key(seed)
        ks = jax.random.split(key, 5)
        s = 0.02
        return {'hidden_states': jax.random.normal(ks[0], (SEQ, BS, H), dtype=jnp.float32), 'router_w': jax.random.normal(ks[1], (H, E), dtype=jnp.float32) * s, 'gate_w': jax.random.normal(ks[2], (E, H, I), dtype=jnp.float32) * s, 'up_w': jax.random.normal(ks[3], (E, H, I), dtype=jnp.float32) * s, 'down_w': jax.random.normal(ks[4], (E, I, H), dtype=jnp.float32) * s}
    _L0_ffn_all = _L0_ffn_setup()
    _L0_ffn_in = {k: v for k, v in _L0_ffn_all.items() if k in ('router_w', 'gate_w', 'up_w', 'down_w')}
    del _L0_ffn_all
    return {'x': x, 'fside_S2_0': fside_S2_0, 'ctx_2048': ctx_2048, 'g_xattn': g_xattn, 'g_ffn': g_ffn, 'L0_xattn_k': _L0_xattn_in['k'], 'L0_ffn_router_w': _L0_ffn_in['router_w'], 'L0_ffn_gate_w': _L0_ffn_in['gate_w'], 'L0_ffn_up_w': _L0_ffn_in['up_w'], 'L0_ffn_down_w': _L0_ffn_in['down_w']}

def reference(x, fside_S2_0, ctx_2048, g_xattn, g_ffn, L0_xattn_k, L0_ffn_router_w, L0_ffn_gate_w, L0_ffn_up_w, L0_ffn_down_w):
    import jax
    import jax.numpy as jnp

    def _L0_xattn_ref(v, k, bias, x1, x2, num_heads):
        import jax, jax.numpy as jnp
        import numpy as np
        B, D, L = v.shape
        H = D // num_heads
        fft_size = 2 * L
        vr = v.reshape(B, H, num_heads, L)
        x1r = x1.reshape(B, H, num_heads, L)
        x2r = x2.reshape(B, H, num_heads, L)
        kv = vr[:, :, :, None, :] * x2r[:, :, None, :, :]
        k_f = jnp.fft.rfft(k.astype(jnp.float32), n=fft_size)
        y = jnp.fft.irfft(jnp.fft.rfft(kv, n=fft_size) * k_f[None, :, None, None, :], n=fft_size)[..., :L]
        skip = bias.astype(jnp.float32).reshape(H, num_heads)[None, :, :, None, None]
        y = y + kv * skip
        out = jnp.einsum('bhijl,bhil->bhjl', y, x1r)
        return out.reshape(B, D, L)

    def _L0_ffn_ref(hidden_states, router_w, gate_w, up_w, down_w):
        import jax, jax.numpy as jnp
        import numpy as np
        SEQ, BS, H, I, E = (512, 4, 512, 1024, 8)
        router_logits = jnp.einsum('sbh,he->sbe', hidden_states, router_w)
        routing_indices = jnp.argmax(router_logits, axis=-1)
        routing_weights = jax.nn.sigmoid(jnp.max(router_logits, axis=-1))
        out = jnp.zeros_like(hidden_states)
        for e in range(E):
            mask = (routing_indices == e)[..., None]
            g = jnp.einsum('sbh,hi->sbi', hidden_states, gate_w[e])
            u = jnp.einsum('sbh,hi->sbi', hidden_states, up_w[e])
            y = jnp.einsum('sbi,ih->sbh', jax.nn.silu(g) * u, down_w[e])
            out = out + jnp.where(mask, y, jnp.zeros((), out.dtype))
        return out
    x = x + jnp.tanh(g_xattn[0]) * _L0_xattn_ref(_layernorm(x, axis=-1), L0_xattn_k, fside_S2_0, ctx_2048, ctx_2048, 8)
    x = x + jnp.tanh(g_ffn[0]) * _L0_ffn_ref(_layernorm(x, axis=-1), L0_ffn_router_w, L0_ffn_gate_w, L0_ffn_up_w, L0_ffn_down_w)
    return x

_drawn_inputs = setup_inputs


def setup_inputs(seed=0):
    import zlib

    import numpy as np

    out = dict(_drawn_inputs(seed))
    spreads = {}
    factors = {'L0_ffn_router_w': 4.076,
     'L0_ffn_gate_w': 3.901,
     'L0_ffn_up_w': 3.817,
     'L0_ffn_down_w': 3.818}
    for name, (base, spread) in spreads.items():
        noise = np.random.default_rng([zlib.crc32(name.encode()), seed]).standard_normal(out[name].shape)
        drawn = base * np.exp(spread * noise) if base else spread * noise
        out[name] = jnp.asarray(drawn.astype(out[name].dtype))
    for name, factor in factors.items():
        out[name] = (out[name] * factor).astype(out[name].dtype)
    return out
```

```python
import concourse.bass as bass
from concourse import mybir
from contextlib import ExitStack


def flamingo_layer_kernel(
    nc: bass.Bass,
    x_rows: bass.AP,
    ctx_cols: bass.AP,
    skip: bass.AP,
    g_xattn: bass.AP,
    g_ffn: bass.AP,
    k: bass.AP,
    router_w: bass.AP,
    gate_w: bass.AP,
    up_w: bass.AP,
    down_w: bass.AP,
    out: bass.AP,
):
    f32 = mybir.dt.float32
    f32r = mybir.dt.float32r
    i32 = mybir.dt.int32
    ALU = mybir.AluOpType
    ACT = mybir.ActivationFunctionType
    AX = mybir.AxisListType.X

    P = 128
    G, _, L = x_rows.shape
    H = k.shape[0]
    J = 8
    NB = P // (2 * J)
    LB = L // P
    COL = NB * J * J
    E, _, I = gate_w.shape
    IB = I // P
    TILES = G + E - 1
    EPS = 1e-5
    KPAD = P + L
    CH = 4
    CW = LB * I // CH
    MW = CH * CW

    kpad = nc.dram_tensor("kpad", [H, KPAD], f32)
    strips = nc.dram_tensor("strips", [H, P, L], f32)
    x2_dram = nc.dram_tensor("x2_dram", [G, P, L], f32)
    xn2_dram = nc.dram_tensor("xn2_dram", [G, P, L], f32)
    sorted_x = nc.dram_tensor("sorted_x", [TILES * P, L], f32)
    sorted_y = nc.dram_tensor("sorted_y", [TILES * P, L], f32)

    base = (nc.sbuf_base + 31) // 32 * 32
    place = [base]

    def put(name, shape, dt=f32, at=None):
        size = 4
        for n in shape[1:]:
            size *= n
        size = (size + 31) // 32 * 32
        if at is None:
            at = place
        t = nc.alloc_sbuf_tensor_at(name, shape, dt, offset=at[0])
        at[0] += size
        return t

    ident = put("ident", [P, P])
    ones = put("ones", [P, P])
    upper = put("upper", [P, P])
    skip_b = put("skip_b", [P, G * 2 * J])
    router = put("router", [P, LB, E])
    e_minus = put("e_minus", [P, E])
    iota_e = put("iota_e", [P, E])
    bounds = put("bounds", [P, G])
    iota_t = put("iota_t", [P, TILES])
    tanh_x = put("tanh_x", [P, 1])
    tanh_f = put("tanh_f", [P, 1])
    logits = put("logits", [P, G, E])
    pos = put("pos", [P, G], i32)
    tile_q = put("tile_q", [1, TILES], i32)
    load_e = put("load_e", [1, E], i32)
    end_q = put("end_q", [1, E], i32)
    mark_pool = put("mark_pool", [P, 1])
    mark_dve = put("mark_dve", [P, 1])
    stats = put("stats", [P, 6])
    mv1 = put("mv1", [P, 2])
    ve1 = put("ve1", [P, 1])
    sd1 = put("sd1", [P, 1])
    rs1 = put("rs1", [P, 1])
    mv2 = put("mv2", [P, 2])
    ve2 = put("ve2", [P, 1])
    sd2 = put("sd2", [P, 1])
    rs2 = put("rs2", [P, 1])
    skip_w = put("skip_w", [P, LB * NB, 2])
    raw = put("raw", [P, CH, CW])
    gate_hi_at = place[0]
    gate_hi = put("gate_hi", [P, 2 * MW], f32r)
    gate_lo_at = place[0]
    gate_lo = put("gate_lo", [P, 2 * MW], f32r)
    up_hi_at = place[0]
    up_hi = put("up_hi", [P, 2 * MW], f32r)
    up_lo = put("up_lo", [P, 2 * MW], f32r)
    down_at = place[0]
    down_hi = put("down_hi", [P, MW], f32r)
    down_lo = put("down_lo", [P, MW], f32r)
    ffn_at = place[0]
    xs = put("xs", [P, L])
    xT_hi = put("xT_hi", [P, LB, P], f32r)
    xT_lo = put("xT_lo", [P, LB, P], f32r)
    silu = put("silu", [P, I])
    hid = put("hid", [P, I])
    hT_hi = put("hT_hi", [P, IB, P], f32r)
    hT_lo = put("hT_lo", [P, IB, P], f32r)
    ys = put("ys", [P, L])

    second = 4 * MW
    a1, a2 = [gate_hi_at + second], [gate_lo_at + second]
    big = [up_hi_at]
    kv = put("kv", [P, 2, LB * COL], f32, a1)
    kv_hi = put("kv_hi", [P, 2, LB * COL], f32r, a2)
    kv_lo = put("kv_lo", [P, 2, LB * COL], f32r, big)
    prod = put("prod", [P, J + 1, LB * P], f32, big)
    t_raw = put("t_raw", [P, 2, L], f32, big)
    t_hi = put("t_hi", [P, 2, 2, L], f32r, big)
    t_lo = put("t_lo", [P, 2, 2, L], f32r, big)
    x_in = put("x_in", [P, 2, L], f32, big)
    x_res = put("x_res", [P, 2, L], f32, big)
    xn = put("xn", [P, L], f32, big)
    xn2 = put("xn2", [P, L], f32, big)
    xn2T = put("xn2T", [P, LB, P], f32, big)
    vT = put("vT", [P, 2, LB * P], f32, big)
    cT = put("cT", [P, 2, LB * P], f32, big)
    vc = put("vc", [P, LB * P], f32, big)
    zero = put("zero", [P, L], f32, big)

    rt = [ffn_at]
    xn_all = put("xn_all", [P, G, L], f32, [down_at])
    best = put("best", [P, G], f32, rt)
    hot = put("hot", [P, G, E], f32, rt)
    cand = put("cand", [P, G, E], f32, rt)
    pick = put("pick", [P, G], f32, rt)
    scan_a = put("scan_a", [P, G, E], f32, rt)
    scan_b = put("scan_b", [P, G, E], f32, rt)
    total = put("total", [P, G, E], f32, rt)
    over = put("over", [P, E, G], f32, rt)
    n_tiles = put("n_tiles", [P, E], f32, rt)
    ends = [put(f"ends{n}", [P, E], f32, rt) for n in range(4)]
    used = put("used", [P, E], f32, rt)
    ranks = [put(f"ranks{n}", [P, E], f32, rt) for n in range(4)]
    base_e = put("base_e", [P, E], f32, rt)
    pos_f = put("pos_f", [P, G], f32, rt)
    match = put("match", [P, E, E], f32, rt)
    match2 = put("match2", [P, E, E], f32, rt)
    sel_e = put("sel_e", [P, E], f32, rt)
    sel_end = put("sel_end", [P, E], f32, rt)
    last_q = put("last_q", [P, E], f32, rt)
    past = put("past", [P, TILES, E], f32, rt)
    tq_f = put("tq_f", [P, TILES], f32, rt)

    fin = [gate_hi_at]
    y_all = put("y_all", [P, G, L], f32, fin)
    x2_all = put("x2_all", [P, G, L], f32, fin)

    ctx = ExitStack()
    with ctx:
        def sem(name):
            return ctx.enter_context(nc.semaphore(name))

        psum = [ctx.enter_context(nc.psum_tensor(f"bank{n}", [P, 512], f32)) for n in range(4)]
        pairs = [ctx.enter_context(nc.psum_tensor(f"pair{n}", [P, 1024], f32)) for n in range(2)]

        y_bank = psum
        v_bank = pairs[0][:, 0:512]
        att_bank = pairs[0][:, 512:1024]
        x2T_bank = pairs[1][:, 0:512]

        s_const = sem("s_const")
        s_kzero = sem("s_kzero")
        s_kcopy = sem("s_kcopy")
        s_strip = [sem(f"s_strip{n}") for n in range(3)]
        s_zfill = sem("s_zfill")
        s_small = sem("s_small")
        s_tanh = sem("s_tanh")
        s_x = [sem(f"s_x{n}") for n in range(2)]
        s_c = [sem(f"s_c{n}") for n in range(2)]
        s_r = [sem(f"s_r{n}") for n in range(2)]
        s_t = sem("s_t")
        s_x2st = [sem(f"s_x2st{n}") for n in range(2)]
        s_xnst = sem("s_xnst")
        s_wraw = [sem(f"s_wraw{n}") for n in range(CH)]
        s_whi = sem("s_whi")
        s_var1 = sem("s_var1")
        s_sd1 = sem("s_sd1")
        s_xn = sem("s_xn")
        s_vtr = sem("s_vtr")
        s_vT = sem("s_vT")
        s_thi = sem("s_thi")
        s_tlo = sem("s_tlo")
        s_kv = sem("s_kv")
        s_khi = sem("s_khi")
        s_klo = sem("s_klo")
        s_skip = sem("s_skip")
        s_skv = sem("s_skv")
        s_skw = sem("s_skw")
        s_skp = sem("s_skp")
        s_y = sem("s_y")
        s_p = sem("s_p")
        s_att = sem("s_att")
        s_x2 = sem("s_x2")
        s_var2 = sem("s_var2")
        s_sd2 = sem("s_sd2")
        s_xn2 = sem("s_xn2")
        s_x2tr = sem("s_x2tr")
        s_xn2T = sem("s_xn2T")
        s_log = sem("s_log")
        s_logc = sem("s_logc")
        s_dve = sem("s_dve")

        def wait(eng, s, value):
            if isinstance(value, int) and value <= 0:
                return
            eng.wait_ge(s, value)

        def stages(eng, body):
            body(0, 0, 0)
            body(1, 1, 0)
            with eng.Fori(1, G // 2 - 1) as pair:
                body(2 * pair, 0, pair)
                body(2 * pair + 1, 1, pair)
            body(G - 2, 0, G // 2 - 1)
            body(G - 1, 1, G // 2 - 1)

        def blk(g, size=1):
            if isinstance(g, int):
                return slice(g * size, (g + 1) * size)
            return bass.ds(g * size, size)

        def known(g, test):
            return test(g) if isinstance(g, int) else True

        s_ready = [sem(f"s_ready_{n}") for n in ("gate", "up", "down")]

        def weight_chunk(kind, e, c):
            if kind < 2:
                w = gate_w if kind == 0 else up_w
                return w[blk(e), c * P:(c + 1) * P, :].rearrange("o p n -> (o p) n")
            rows = down_w[blk(e), 2 * c * P:(2 * c + 2) * P, :]
            return rows.rearrange("o (k p) n -> p (o k) n", p=P)

        def raw_chunk(kind, c):
            return raw[:, c, :] if kind < 2 else raw[:, c, :].rearrange("p (k n) -> p k n", k=2)

        GATE, UP, DOWN = range(3)

        def load_matrix(eng, kind, e, before=None, q_before=0):
            for c in range(CH):
                if before is not None:
                    eng.wait_ge(s_ready[before], q_before * CH + (c + 1))
                eng.dma_start(raw_chunk(kind, c), weight_chunk(kind, e, c)).then_inc(s_wraw[c], 16)


        def split_matrix(eng, kind, slot, count, chunks=range(CH)):
            hi, lo = ((gate_hi, gate_lo), (up_hi, up_lo), (down_hi, down_lo))[kind]
            offset = slot * MW
            for c in chunks:
                a, b = offset + c * CW, offset + (c + 1) * CW
                eng.wait_ge(s_wraw[c], (count + 1) * 16)
                nc.gpsimd.tensor_tensor(mark_pool[:, :], ones[:, 0:1], ones[:, 0:1], ALU.mult)
                nc.gpsimd.tensor_scalar(hi[:, a:b], raw[:, c, :], 1.0, 1.0, ALU.mult, ALU.mult).then_inc(s_whi, 1)
                eng.wait_ge(s_whi, count * CH + (c + 1))
                nc.gpsimd.tensor_tensor(lo[:, a:b], raw[:, c, :], hi[:, a:b].bitcast(f32),
                                        ALU.subtract).then_inc(s_ready[kind], 1)

        with nc.Block() as block:

            @block.sync
            def _(eng):
                eng.dma_start(kpad[:, P:KPAD], k).then_inc(s_kcopy, 16)
                eng.dma_start(skip_b[:, :], bass.AP(skip.tensor, 0, [[0, P], [1, G * 2 * J]])).then_inc(s_small, 16)
                eng.dma_start(router[:, :, :], router_w.rearrange("(b p) e -> p b e", p=P)).then_inc(s_small, 16)
                eng.dma_start(tanh_x[:, :], bass.AP(g_xattn.tensor, 0, [[0, P], [1, 1]])).then_inc(s_small, 16)
                eng.dma_start(tanh_f[:, :], bass.AP(g_ffn.tensor, 0, [[0, P], [1, 1]])).then_inc(s_small, 16)
                eng.wait_ge(s_const, 1)
                eng.dma_start(kpad[:, 0:P], zero[0:H, 0:P]).then_inc(s_kzero, 16)
                eng.wait_ge(s_kcopy, 16)
                eng.wait_ge(s_kzero, 16)
                for n, (g0, g1) in enumerate(((0, 1), (1, 2), (2, G))):
                    eng.dma_start(strips[2 * g0:2 * g1, :, :],
                                  bass.AP(kpad, 2 * g0 * KPAD + P, [[KPAD, 2 * (g1 - g0)], [-1, P], [1, L]]))\
                       .then_inc(s_strip[n], 16)

                def store_x2(g, u, n):
                    eng.wait_ge(s_x2, g + 1)
                    eng.dma_start(x2_dram[blk(g), :, :].rearrange("o p n -> (o p) n"),
                                  x_res[:, u, :]).then_inc(s_x2st[u], 16)

                def store_xn2(g):
                    eng.wait_ge(s_xn2, g + 1)
                    eng.dma_start(xn2_dram[blk(g), :, :].rearrange("o p n -> (o p) n"),
                                  xn2[:, :]).then_inc(s_xnst, 16)

                def stage(g, u, n):
                    wait(eng, s_xn, g - 1)
                    eng.dma_start(x_in[:, u, :], x_rows[blk(g), :, :].rearrange("o p n -> (o p) n"))\
                       .then_inc(s_x[u], 16)
                    wait(eng, s_p, (g - 1) * 2 * LB)
                    wait(eng, s_skp, g - 1)
                    wait(eng, s_kv, 2 * (g - 1))
                    eng.dma_start(cT[:, u, :], ctx_cols[blk(g), :, :].rearrange("o p n -> (o p) n"))\
                       .then_inc(s_c[u], 16)
                    wait(eng, s_thi, g)
                    wait(eng, s_tlo, g)
                    n_strip = min(g, 2) if isinstance(g, int) else 2
                    eng.wait_ge(s_strip[n_strip], 16)
                    eng.dma_start(t_raw[:, :, :], strips[blk(g, 2), :, :].rearrange("h p n -> p h n"))\
                       .then_inc(s_t, 16)
                    if known(g, lambda g: g >= 2):
                        store_x2(g - 2, u, n)
                        store_xn2(g - 2)
                        eng.wait_ge(s_x2st[u], 16 * n)
                    eng.dma_start(x_res[:, u, :], x_rows[blk(g), :, :].rearrange("o p n -> (o p) n"))\
                       .then_inc(s_r[u], 16)
                    if isinstance(g, int) and g == 1:
                        load_matrix(eng, GATE, 0)
                        for t in range(TILES):
                            eng.dma_start(sorted_x[t * P:(t + 1) * P, :], zero[:, :]).then_inc(s_zfill, 16)

                stages(eng, stage)
                for g in (G - 2, G - 1):
                    store_x2(g, g % 2, 0)
                    store_xn2(g)
                for u in range(2):
                    eng.wait_ge(s_x2st[u], 16 * (G // 2))
                eng.wait_ge(s_xnst, 16 * G)
                eng.wait_ge(s_zfill, 16 * TILES)

            @block.gpsimd
            def _(eng):
                nc.gpsimd.memset(zero[:, :], 0.0).then_inc(s_const, 1)
                nc.gpsimd.memset(ident[:, :], 0.0).then_inc(s_const, 1)
                nc.gpsimd.memset(ones[:, :], 1.0).then_inc(s_const, 1)
                eng.wait_ge(s_const, 3)
                nc.gpsimd.affine_select(out=ident[:, :], in_=ident[:, :], compare_op=ALU.not_equal, fill=1.0,
                                        base=0, pattern=[[-1, P]], channel_multiplier=1).then_inc(s_const, 1)
                nc.gpsimd.affine_select(out=upper[:, :], in_=ones[:, :], compare_op=ALU.is_gt, fill=0.0,
                                        base=0, pattern=[[1, P]], channel_multiplier=-1).then_inc(s_const, 1)
                for t, base0, step in ((e_minus, 1 - E, 1), (iota_e, 0, 1), (bounds, 0, P), (iota_t, 0, 1)):
                    nc.gpsimd.iota(t[:, :], pattern=[[step, t.shape[1]]], base=base0, channel_multiplier=0,
                                   allow_small_or_imprecise_dtypes=True).then_inc(s_const, 1)

                def outer(u, hh, g, n):
                    h = 2 * g + hh
                    if hh == 0:
                        eng.wait_ge(s_vT, g + 1)
                        eng.wait_ge(s_c[u], 16 * (n + 1))
                    wait(eng, s_khi, h - 1)
                    wait(eng, s_klo, h - 1)
                    v = vT[:, u, :].rearrange("p (a r) -> p a r", r=2 * J)[:, :, hh * J:(hh + 1) * J]
                    c = cT[:, u, :].rearrange("p (a r) -> p a r", r=2 * J)[:, :, hh * J:(hh + 1) * J]
                    nc.gpsimd.tensor_tensor(
                        kv[:, hh, :].rearrange("p (a i j) -> p a i j", i=J, j=J),
                        v.unsqueeze(3).broadcast_to([P, LB * NB, J, J]),
                        c.unsqueeze(2).broadcast_to([P, LB * NB, J, J]), ALU.mult).then_inc(s_kv, 1)

                def skip_first(g, u):
                    a = LB * NB
                    wait(eng, s_skw, g)
                    wait(eng, s_skip, g)
                    s_g = skip_b[:, blk(g, 2 * J)]
                    nc.gpsimd.tensor_tensor(
                        vc[:, :].rearrange("p (a r) -> p a r", r=2 * J),
                        vT[:, u, :].rearrange("p (a r) -> p a r", r=2 * J),
                        s_g.unsqueeze(1).broadcast_to([P, a, 2 * J]), ALU.mult).then_inc(s_skv, 1)
                    eng.wait_ge(s_skv, g + 1)
                    nc.gpsimd.tensor_tensor(vc[:, :], vc[:, :], cT[:, u, :], ALU.mult).then_inc(s_skip, 1)

                def skip_last(g, u):
                    eng.wait_ge(s_skw, g + 1)
                    wait(eng, s_att, g)
                    nc.gpsimd.tensor_tensor(
                        prod[:, J, :].rearrange("p (a h j) -> p a h j", h=2, j=J),
                        cT[:, u, :].rearrange("p (a h j) -> p a h j", h=2, j=J),
                        skip_w[:, :, :].unsqueeze(3).broadcast_to([P, LB * NB, 2, J]), ALU.mult)\
                        .then_inc(s_skp, 1)

                def stage(g, u, n):
                    outer(u, 1, g, n)
                    skip_first(g, u)
                    if known(g, lambda g: g < G - 1):
                        outer(1 - u, 0, g + 1, n + u)
                    skip_last(g, u)
                    if isinstance(g, int) and g in (G - 2, G - 1):
                        split_matrix(eng, GATE, 0, 0, range(2 * u, 2 * u + 2))

                eng.wait_ge(s_small, 64)
                outer(0, 0, 0, 0)
                stages(eng, stage)

            @block.scalar
            def _(act):
                def root1(g):
                    act.wait_ge(s_var1, g + 1)
                    nc.scalar.activation(sd1[:, :], ve1[:, :], ACT.Sqrt).then_inc(s_sd1, 1)

                def strip_hi(g, u):
                    act.wait_ge(s_t, 16 * (g + 1))
                    wait(act, s_y, (g - 1) * 2 * LB)
                    nc.scalar.activation(t_hi[:, u, :, :], t_raw[:, :, :], ACT.Copy).then_inc(s_thi, 1)

                def v_out(g, u):
                    act.wait_ge(s_vtr, g + 1)
                    wait(act, s_kv, 2 * (g - 1))
                    wait(act, s_skip, g - 1)
                    nc.scalar.activation(vT[:, u, :], v_bank, ACT.Copy).then_inc(s_vT, 1)

                def kv_high(h, hh):
                    act.wait_ge(s_kv, h + 1)
                    wait(act, s_y, (h - 1) * LB)
                    nc.scalar.activation(kv_hi[:, hh, :], kv[:, hh, :], ACT.Copy).then_inc(s_khi, 1)

                def logits_out(g):
                    act.wait_ge(s_log, g + 1)
                    nc.scalar.activation(logits[:, blk(g), :].rearrange("p o e -> p (o e)"),
                                         att_bank[:, 0:E], ACT.Copy).then_inc(s_logc, 1)

                def root2(g):
                    act.wait_ge(s_var2, g + 1)
                    nc.scalar.activation(sd2[:, :], ve2[:, :], ACT.Sqrt).then_inc(s_sd2, 1)

                def xn2T_out(g):
                    act.wait_ge(s_x2tr, g + 1)
                    wait(act, s_log, g)
                    nc.scalar.activation(xn2T[:, :, :].rearrange("p b t -> p (b t)"), x2T_bank, ACT.Copy)\
                        .then_inc(s_xn2T, 1)

                def stage(g, u, n):
                    kv_high(2 * g + 1, 1)
                    more = known(g, lambda g: g < G - 1)
                    if more:
                        root1(g + 1)
                    if known(g, lambda g: g >= 2):
                        logits_out(g - 2)
                    if more:
                        strip_hi(g + 1, 1 - u)
                        v_out(g + 1, 1 - u)
                    if known(g, lambda g: g >= 1):
                        root2(g - 1)
                    if more:
                        kv_high(2 * g + 2, 0)
                    if known(g, lambda g: g >= 1):
                        xn2T_out(g - 1)

                act.wait_ge(s_small, 64)
                nc.scalar.activation(tanh_x[:, :], tanh_x[:, :], ACT.Tanh).then_inc(s_tanh, 1)
                nc.scalar.activation(tanh_f[:, :], tanh_f[:, :], ACT.Tanh).then_inc(s_tanh, 1)
                root1(0)
                strip_hi(0, 0)
                v_out(0, 0)
                kv_high(0, 0)
                stages(act, stage)
                logits_out(G - 2)
                root2(G - 1)
                xn2T_out(G - 1)
                logits_out(G - 1)

            @block.vector
            def _(dve):
                LN_STEPS = 2

                def norm_first(src, mv, ve, done, count):
                    nc.vector.bn_stats(stats[:, :], src).then_inc(s_dve, 1)
                    dve.wait_ge(s_dve, count + 1)
                    nc.vector.tensor_copy(mark_dve[:, :], stats[:, 0:1])
                    nc.vector.bn_aggr(mv[:, :], stats[:, :]).then_inc(s_dve, 1)
                    dve.wait_ge(s_dve, count + 2)
                    nc.vector.tensor_scalar(ve[:, :], mv[:, 1:2], EPS, None, ALU.add).then_inc(done, 1)

                def norm_last(dst, src, mv, sd, rs, s_sd, g, count, done):
                    dve.wait_ge(s_sd, g + 1)
                    nc.vector.reciprocal(rs[:, :], sd[:, :]).then_inc(s_dve, 1)
                    dve.wait_ge(s_dve, count + 1)
                    nc.vector.tensor_scalar(dst, src, mv[:, 0:1], rs[:, 0:1], ALU.subtract, ALU.mult)\
                        .then_inc(done, 1)

                def steps_before(g):
                    return 3 + 6 * g - 3

                def ln1_first(g, u, n, count):
                    dve.wait_ge(s_x[u], 16 * (n + 1))
                    norm_first(x_in[:, u, :], mv1, ve1, s_var1, count)

                def ln1_last(g, u, count):
                    wait(dve, s_vtr, g)
                    norm_last(xn[:, :], x_in[:, u, :], mv1, sd1, rs1, s_sd1, g, count, s_xn)

                def strip_lo(g, u):
                    dve.wait_ge(s_thi, g + 1)
                    wait(dve, s_y, (g - 1) * 2 * LB)
                    nc.vector.tensor_tensor(t_lo[:, u, :, :], t_raw[:, :, :], t_hi[:, u, :, :].bitcast(f32),
                                            ALU.subtract).then_inc(s_tlo, 1)

                def kv_low(h, hh):
                    dve.wait_ge(s_khi, h + 1)
                    wait(dve, s_y, (h - 1) * LB)
                    nc.vector.tensor_tensor(kv_lo[:, hh, :], kv[:, hh, :], kv_hi[:, hh, :].bitcast(f32),
                                            ALU.subtract).then_inc(s_klo, 1)

                def products(g, u, hh):
                    h = 2 * g + hh
                    if hh == 0:
                        wait(dve, s_att, g)
                    for lb in range(LB):
                        dve.wait_ge(s_y, h * LB + lb + 1)
                        c = cT[:, u, lb * P:(lb + 1) * P].rearrange("p (b r) -> p b r", r=2 * J)
                        c = c[:, :, hh * J:(hh + 1) * J].unsqueeze(3).broadcast_to([P, NB, J, J])
                        dst = prod[:, 0:J, lb * P:(lb + 1) * P].rearrange("p i (b r) -> p b i r", r=2 * J)
                        nc.vector.tensor_tensor(dst[:, :, :, hh * J:(hh + 1) * J],
                                                y_bank[lb][:, :].rearrange("p (b i j) -> p b i j", i=J, j=J),
                                                c, ALU.mult).then_inc(s_p, 1)

                def residual(g, u, n):
                    dve.wait_ge(s_att, g + 1)
                    dve.wait_ge(s_r[u], 16 * (n + 1))
                    nc.vector.scalar_tensor_tensor(out=x_res[:, u, :], in0=att_bank, scalar=tanh_x[:, 0:1],
                                                   in1=x_res[:, u, :], op0=ALU.mult, op1=ALU.add)\
                        .then_inc(s_x2, 1)

                def ln2_first(g, u, count):
                    dve.wait_ge(s_x2, g + 1)
                    norm_first(x_res[:, u, :], mv2, ve2, s_var2, count)

                def ln2_last(g, u, count):
                    wait(dve, s_x2tr, g)
                    wait(dve, s_xnst, 16 * g)
                    norm_last(xn2[:, :], x_res[:, u, :], mv2, sd2, rs2, s_sd2, g, count, s_xn2)

                def skip_sum(g):
                    dve.wait_ge(s_skip, g + 1)
                    wait(dve, s_skp, g)
                    nc.vector.tensor_reduce(skip_w[:, :, :],
                                            vc[:, :].rearrange("p (a h i) -> p a h i", h=2, i=J), AX, ALU.add)\
                        .then_inc(s_skw, 1)

                def stage(g, u, n):
                    more = known(g, lambda g: g < G - 1)
                    before = known(g, lambda g: g >= 1)
                    count = steps_before(g) if not isinstance(g, int) else (3 if g == 0 else steps_before(g))
                    if more:
                        ln1_first(g + 1, 1 - u, n + u, count)
                    kv_low(2 * g + 1, 1)
                    if more:
                        ln1_last(g + 1, 1 - u, count + 2)
                        strip_lo(g + 1, 1 - u)
                        count = count + 3
                    products(g, u, 0)
                    if before:
                        residual(g - 1, 1 - u, n - 1 + u)
                        ln2_first(g - 1, 1 - u, count)
                    skip_sum(g)
                    if before:
                        ln2_last(g - 1, 1 - u, count + 2)
                    if more:
                        kv_low(2 * g + 2, 0)
                    products(g, u, 1)

                ln1_first(0, 0, 0, 0)
                ln1_last(0, 0, 2)
                strip_lo(0, 0)
                kv_low(0, 0)
                dve.wait_ge(s_tanh, 2)
                stages(dve, stage)
                count = steps_before(G - 1) + 3
                residual(G - 1, 1, G // 2 - 1)
                ln2_first(G - 1, 1, count)
                ln2_last(G - 1, 1, count + 2)

            @block.tensor
            def _(pe):
                def transposes(bank, src, done):
                    for b in range(LB):
                        last = nc.tensor.transpose(bank[:, b * P:(b + 1) * P], src[:, b * P:(b + 1) * P],
                                                   ident[:, :])
                    last.then_inc(done, 1)

                def v_in(g):
                    pe.wait_ge(s_xn, g + 1)
                    wait(pe, s_vT, g)
                    transposes(v_bank, xn, s_vtr)

                def conv(g, u, hh, blocks):
                    h = 2 * g + hh
                    for lb in blocks:
                        if lb == 0:
                            pe.wait_ge(s_klo, h + 1)
                            if hh == 0:
                                pe.wait_ge(s_tlo, g + 1)
                        wait(pe, s_p, (h - 1) * LB + lb + 1)
                        for mb in range(lb + 1):
                            d = lb - mb
                            for n, (t, v) in enumerate(((t_hi, kv_hi), (t_hi, kv_lo), (t_lo, kv_hi))):
                                last = nc.tensor.matmul(
                                    y_bank[lb][:, :], t[:, u, hh, d * P:(d + 1) * P],
                                    v[:, hh, mb * COL:(mb + 1) * COL],
                                    start=(mb == 0 and n == 0), stop=(mb == lb and n == 2))
                        last.then_inc(s_y, 1)

                def logits_of(g):
                    pe.wait_ge(s_xn2T, g + 1)
                    pe.wait_ge(s_x2, g + 1)
                    for b in range(LB):
                        last = nc.tensor.matmul(att_bank[:, 0:E], xn2T[:, b, :], router[:, b, :],
                                                start=(b == 0), stop=(b == LB - 1))
                    last.then_inc(s_log, 1)

                def sum_heads(g):
                    pe.wait_ge(s_p, (g + 1) * 2 * LB)
                    pe.wait_ge(s_skp, g + 1)
                    wait(pe, s_x2, g)
                    wait(pe, s_logc, g)
                    for lb in range(LB):
                        for i in range(J + 1):
                            last = nc.tensor.matmul(att_bank[:, lb * P:(lb + 1) * P],
                                                    prod[:, i, lb * P:(lb + 1) * P], ident[:, :],
                                                    start=(i == 0), stop=(i == J), is_transpose=True)
                    last.then_inc(s_att, 1)

                def x2_in(g):
                    pe.wait_ge(s_xn2, g + 1)
                    wait(pe, s_xn2T, g)
                    transposes(x2T_bank, xn2, s_x2tr)

                def stage(g, u, n):
                    conv(g, u, 0, (0, 1))
                    if known(g, lambda g: g >= 2):
                        logits_of(g - 2)
                    if known(g, lambda g: g < G - 1):
                        v_in(g + 1)
                    if known(g, lambda g: g >= 1):
                        sum_heads(g - 1)
                    conv(g, u, 0, (2, 3))
                    conv(g, u, 1, (0, 1))
                    if known(g, lambda g: g >= 1):
                        x2_in(g - 1)
                    conv(g, u, 1, (2, 3))

                pe.wait_ge(s_const, 5)
                v_in(0)
                stages(pe, stage)
                logits_of(G - 2)
                sum_heads(G - 1)
                x2_in(G - 1)
                logits_of(G - 1)

        s_xall = [sem(f"s_xall{n}") for n in range(4)]
        s_hot = sem("s_hot")
        s_cnt = sem("s_cnt")
        s_pos = sem("s_pos")
        s_tab = sem("s_tab")
        s_scat = [sem(f"s_scat{n}") for n in range(G)]
        s_rt = sem("s_rt")

        with nc.Block() as block:

            @block.sync
            def _(eng):
                load_matrix(eng, UP, 0, GATE, 0)
                for n in range(4):
                    q = G // 4
                    eng.dma_start(xn_all[:, n * q:(n + 1) * q, :],
                                  xn2_dram[n * q:(n + 1) * q, :, :].rearrange("g p n -> p g n")).then_inc(s_xall[n], 16)

            @block.tensor
            def _(pe):
                pe.wait_ge(s_hot, 1)
                flat = hot[:, :, :].rearrange("p g e -> p (g e)")
                nc.tensor.matmul(psum[0][:, 0:G * E], upper[:, :], flat, start=True, stop=True)
                nc.tensor.matmul(psum[1][:, 0:G * E], ones[:, :], flat, start=True, stop=True).then_inc(s_cnt, 1)

            @block.vector
            def _(dve):
                done = [0]

                def step(instruction):
                    done[0] += 1
                    instruction.then_inc(s_rt, 1)
                    dve.wait_ge(s_rt, done[0])

                V = nc.vector
                ge = [P, G, E]
                step(V.tensor_reduce(best[:, :], logits[:, :, :], AX, ALU.max))
                step(V.tensor_tensor(cand[:, :, :], logits[:, :, :], best[:, :].unsqueeze(2).broadcast_to(ge),
                                     ALU.is_equal))
                step(V.tensor_tensor(hot[:, :, :], cand[:, :, :], e_minus[:, :].unsqueeze(1).broadcast_to(ge),
                                     ALU.mult))
                step(V.tensor_reduce(pick[:, :], hot[:, :, :], AX, ALU.min))
                V.tensor_tensor(hot[:, :, :], e_minus[:, :].unsqueeze(1).broadcast_to(ge),
                                pick[:, :].unsqueeze(2).broadcast_to(ge), ALU.is_equal).then_inc(s_hot, 1)
                dve.wait_ge(s_cnt, 1)
                step(V.tensor_copy(total[:, :, :], psum[1][:, 0:G * E].rearrange("p (g e) -> p g e", e=E)))
                src, dst = total, scan_a
                shift = 1
                while shift < G:
                    V.tensor_copy(dst[:, 0:shift, :], src[:, 0:shift, :])
                    step(V.tensor_tensor(dst[:, shift:G, :], src[:, shift:G, :], src[:, 0:G - shift, :], ALU.add))
                    src, dst = dst, (scan_b if dst is scan_a else scan_a)
                    shift *= 2
                counts = src[:, G - 1, :]
                step(V.tensor_tensor(over[:, :, :], counts.unsqueeze(2).broadcast_to([P, E, G]),
                                     bounds[:, :].unsqueeze(1).broadcast_to([P, E, G]), ALU.is_gt))
                step(V.tensor_reduce(n_tiles[:, :], over[:, :, :], AX, ALU.add))
                step(V.tensor_scalar(n_tiles[:, 0:1], n_tiles[:, 0:1], 1.0, None, ALU.max))
                step(V.tensor_scalar(used[:, :], n_tiles[:, :], 0.0, None, ALU.is_gt))
                step(V.tensor_copy(ends[0][:, :], n_tiles[:, :]))
                step(V.tensor_copy(ranks[0][:, :], used[:, :]))
                for n, shift in enumerate((1, 2, 4)):
                    for s in (ends, ranks):
                        V.tensor_copy(s[n + 1][:, 0:shift], s[n][:, 0:shift])
                        step(V.tensor_tensor(s[n + 1][:, shift:E], s[n][:, shift:E], s[n][:, 0:E - shift], ALU.add))
                end_e, rank_e = ends[3], ranks[3]
                step(V.tensor_tensor(base_e[:, :], end_e[:, :], n_tiles[:, :], ALU.subtract))
                step(V.tensor_scalar(base_e[:, :], base_e[:, :], float(P), None, ALU.mult))
                step(V.tensor_tensor(dst[:, :, :], src[:, :, :], total[:, :, :], ALU.subtract))
                step(V.tensor_tensor(dst[:, :, :], psum[0][:, 0:G * E].rearrange("p (g e) -> p g e", e=E),
                                     dst[:, :, :], ALU.add))
                step(V.tensor_tensor(dst[:, :, :], dst[:, :, :], base_e[:, :].unsqueeze(1).broadcast_to(ge), ALU.add))
                step(V.tensor_tensor(dst[:, :, :], dst[:, :, :], hot[:, :, :], ALU.mult))
                step(V.tensor_reduce(pos_f[:, :], dst[:, :, :], AX, ALU.add))
                V.tensor_copy(pos[:, :], pos_f[:, :]).then_inc(s_pos, 1)
                ee = [P, E, E]
                step(V.tensor_scalar(last_q[:, :], iota_e[:, :], rank_e[:, E - 1:E], -1.0, ALU.subtract, ALU.is_ge))
                step(V.tensor_scalar(last_q[:, :], last_q[:, :], float(TILES), None, ALU.mult))
                step(V.tensor_scalar(rank_e[:, :], rank_e[:, :], -1.0, None, ALU.add))
                step(V.tensor_tensor(match[:, :, :], rank_e[:, :].unsqueeze(1).broadcast_to(ee),
                                     iota_e[:, :].unsqueeze(2).broadcast_to(ee), ALU.is_equal))
                step(V.tensor_tensor(match[:, :, :], match[:, :, :], used[:, :].unsqueeze(1).broadcast_to(ee),
                                     ALU.mult))
                step(V.tensor_tensor(match2[:, :, :], match[:, :, :], iota_e[:, :].unsqueeze(1).broadcast_to(ee),
                                     ALU.mult))
                step(V.tensor_reduce(sel_e[:, :], match2[:, :, :], AX, ALU.add))
                step(V.tensor_tensor(match2[:, :, :], match[:, :, :], end_e[:, :].unsqueeze(1).broadcast_to(ee),
                                     ALU.mult))
                step(V.tensor_reduce(sel_end[:, :], match2[:, :, :], AX, ALU.add))
                step(V.tensor_tensor(sel_end[:, :], sel_end[:, :], last_q[:, :], ALU.max))
                te = [P, TILES, E]
                step(V.tensor_tensor(past[:, :, :], iota_t[:, :].unsqueeze(2).broadcast_to(te),
                                     sel_end[:, :].unsqueeze(1).broadcast_to(te), ALU.is_ge))
                step(V.tensor_reduce(tq_f[:, :], past[:, :, :], AX, ALU.add))
                V.tensor_copy(load_e[:, :], sel_e[0:1, :])
                V.tensor_copy(end_q[:, :], sel_end[0:1, :])
                V.tensor_copy(tile_q[:, :], tq_f[0:1, :]).then_inc(s_tab, 1)

            @block.gpsimd
            def _(eng):
                split_matrix(eng, UP, 0, 1)
                eng.wait_ge(s_pos, 1)
                for g in range(G):
                    if g % (G // 4) == 0:
                        eng.wait_ge(s_xall[g // (G // 4)], 16)
                    nc.gpsimd.indirect_dma_start(
                        out=sorted_x[:, :], out_offset=bass.IndirectOffsetOnAxis(ap=pos[:, g:g + 1], axis=0),
                        in_=xn_all[:, g, :], in_offset=None).then_inc(s_scat[g], 16)
                for g in range(G):
                    eng.wait_ge(s_scat[g], 16)

        gate_bank = pairs[0]
        up_bank = pairs[1]
        x_bank, out_bank = psum[0], psum[1]
        h_bank = psum[2:4]
        s_xs = sem("s_xs")
        s_xtr = sem("s_xtr")
        s_xhi = sem("s_xhi")
        s_xlo = sem("s_xlo")
        s_gate = sem("s_gate")
        s_up = sem("s_up")
        s_down = sem("s_down")
        s_silu = sem("s_silu")
        s_hid = sem("s_hid")
        s_htr = sem("s_htr")
        s_hhi = sem("s_hhi")
        s_hlo = sem("s_hlo")
        s_ys = sem("s_ys")
        s_yst = sem("s_yst")

        FIRST = 5

        def tiles(eng, body):
            body(0)
            with eng.Fori(1, TILES - 1) as t:
                body(t)
            body(TILES - 1)

        with nc.Block() as block:

            @block.sync
            def _(eng):
                def expert(q):
                    return eng.value_load(load_e[0:1, blk(q)], min_val=0, max_val=E - 1)

                load_matrix(eng, DOWN, 0, UP, 0)
                second_e = expert(1)
                load_matrix(eng, GATE, second_e, DOWN, 0)
                load_matrix(eng, UP, second_e, GATE, 1)

                def load_three(q, before, q_before):
                    ahead = expert(q + 2)
                    load_matrix(eng, GATE, ahead, before, q_before)
                    load_matrix(eng, UP, ahead, GATE, q + 2)
                    load_matrix(eng, DOWN, expert(q + 1), UP, q + 2)

                load_three(0, UP, 1)
                with eng.Fori(1, E - 2) as q:
                    load_three(q, DOWN, q)
                load_matrix(eng, DOWN, expert(E - 1), DOWN, E - 2)

            @block.gpsimd
            def _(eng):
                split_matrix(eng, DOWN, 0, 2)
                split_matrix(eng, GATE, 1, 3)
                split_matrix(eng, UP, 1, 4)
                with eng.Fori(0, E // 2 - 1) as pair:
                    for u in range(2):
                        q = 2 * pair + u
                        end = eng.value_load(end_q[0:1, blk(q)], min_val=1, max_val=TILES)
                        eng.wait_ge(s_gate, end)
                        split_matrix(eng, GATE, u, 3 * q + FIRST)
                        eng.wait_ge(s_up, end)
                        split_matrix(eng, UP, u, 3 * q + (FIRST + 1))
                        eng.wait_ge(s_down, end)
                        split_matrix(eng, DOWN, 0, 3 * q + (FIRST + 2))
                end = eng.value_load(end_q[0:1, E - 2:E - 1], min_val=1, max_val=TILES)
                eng.wait_ge(s_down, end)
                split_matrix(eng, DOWN, 0, 3 * E - 1)

            @block.scalar
            def _(act):
                def load(t):
                    act.dma_start(xs[:, :], sorted_x[blk(t, P), :]).then_inc(s_xs, 16)

                def high_x(t):
                    act.wait_ge(s_xtr, t + 1)
                    nc.scalar.activation(xT_hi[:, :, :].rearrange("p b t -> p (b t)"), x_bank[:, :], ACT.Copy)\
                        .then_inc(s_xhi, 1)

                def out_tile(t):
                    act.wait_ge(s_down, t + 1)
                    wait(act, s_yst, 16 * t)
                    nc.scalar.activation(ys[:, :], out_bank[:, :], ACT.Copy, scale=tanh_f[:, 0:1]).then_inc(s_ys, 1)
                    act.wait_ge(s_ys, t + 1)
                    act.dma_start(sorted_y[blk(t, P), :], ys[:, :]).then_inc(s_yst, 16)

                def tile(t):
                    act.wait_ge(s_gate, t + 1)
                    wait(act, s_hid, t)
                    nc.scalar.activation(silu[:, :], gate_bank[:, :], ACT.Silu).then_inc(s_silu, 1)
                    if known(t, lambda t: t < TILES - 1):
                        high_x(t + 1)
                    if known(t, lambda t: t < TILES - 2):
                        load(t + 2)
                    if known(t, lambda t: t > 0):
                        out_tile(t - 1)
                    act.wait_ge(s_htr, t + 1)
                    for n in range(2):
                        last = nc.scalar.activation(
                            hT_hi[:, n * LB:(n + 1) * LB, :].rearrange("p b t -> p (b t)"), h_bank[n][:, :], ACT.Copy)
                    last.then_inc(s_hhi, 1)

                load(0)
                high_x(0)
                load(1)
                tile(0)
                with act.Fori(1, TILES - 2) as t:
                    tile(t)
                tile(TILES - 2)
                tile(TILES - 1)
                out_tile(TILES - 1)
                act.wait_ge(s_yst, 16 * TILES)

            @block.vector
            def _(dve):
                def low_x(t):
                    dve.wait_ge(s_xhi, t + 1)
                    nc.vector.tensor_tensor(xT_lo[:, :, :].rearrange("p b t -> p (b t)"), x_bank[:, :],
                                            xT_hi[:, :, :].rearrange("p b t -> p (b t)").bitcast(f32),
                                            ALU.subtract).then_inc(s_xlo, 1)

                def tile(t):
                    dve.wait_ge(s_silu, t + 1)
                    dve.wait_ge(s_up, t + 1)
                    wait(dve, s_htr, t)
                    nc.vector.tensor_tensor(hid[:, :], up_bank[:, :], silu[:, :], ALU.mult).then_inc(s_hid, 1)
                    if known(t, lambda t: t < TILES - 1):
                        low_x(t + 1)
                    dve.wait_ge(s_hhi, t + 1)
                    for n in range(2):
                        last = nc.vector.tensor_tensor(
                            hT_lo[:, n * LB:(n + 1) * LB, :].rearrange("p b t -> p (b t)"), h_bank[n][:, :],
                            hT_hi[:, n * LB:(n + 1) * LB, :].rearrange("p b t -> p (b t)").bitcast(f32),
                            ALU.subtract)
                    last.then_inc(s_hlo, 1)

                low_x(0)
                tiles(dve, tile)

            @block.tensor
            def _(pe):
                def expert_of(t):
                    return pe.value_load(tile_q[0:1, blk(t)], min_val=0, max_val=E - 1)

                def x_in_array(t):
                    pe.wait_ge(s_xs, 16 * (t + 1))
                    wait(pe, s_xlo, t)
                    for b in range(LB):
                        last = nc.tensor.transpose(x_bank[:, b * P:(b + 1) * P], xs[:, b * P:(b + 1) * P],
                                                   ident[:, :])
                    last.then_inc(s_xtr, 1)

                def project(bank, hi, lo, slot, done):
                    for half in range(I // 512):
                        for b in range(LB):
                            o = slot * MW + (b * I + half * 512)
                            for n, (a, w) in enumerate(((xT_hi, hi), (xT_hi, lo), (xT_lo, hi))):
                                last = nc.tensor.matmul(bank[:, half * 512:(half + 1) * 512], a[:, b, :],
                                                        w[:, bass.ds(o, 512)],
                                                        start=(b == 0 and n == 0), stop=(b == LB - 1 and n == 2))
                    last.then_inc(done, 1)

                def down(t):
                    q = expert_of(t)
                    pe.wait_ge(s_hlo, t + 1)
                    wait(pe, s_ys, t)
                    for b in range(IB):
                        if b % 2 == 0:
                            pe.wait_ge(s_ready[DOWN], q * CH + (b // 2 + 1))
                        for n, (a, w) in enumerate(((hT_hi, down_hi), (hT_hi, down_lo), (hT_lo, down_hi))):
                            last = nc.tensor.matmul(out_bank[:, :], a[:, b, :], w[:, b * 512:(b + 1) * 512],
                                                    start=(b == 0 and n == 0), stop=(b == IB - 1 and n == 2))
                    last.then_inc(s_down, 1)

                def tile(t):
                    q = expert_of(t)
                    slot = q % 2
                    pe.wait_ge(s_xlo, t + 1)
                    wait(pe, s_silu, t)
                    pe.wait_ge(s_ready[GATE], (q + 1) * CH)
                    project(gate_bank, gate_hi, gate_lo, slot, s_gate)
                    wait(pe, s_hid, t)
                    pe.wait_ge(s_ready[UP], (q + 1) * CH)
                    project(up_bank, up_hi, up_lo, slot, s_up)
                    if known(t, lambda t: t < TILES - 1):
                        x_in_array(t + 1)
                    if known(t, lambda t: t > 0):
                        down(t - 1)
                    pe.wait_ge(s_hid, t + 1)
                    wait(pe, s_hlo, t)
                    for b in range(IB):
                        last = nc.tensor.transpose(h_bank[b // LB][:, (b % LB) * P:(b % LB + 1) * P],
                                                   hid[:, b * P:(b + 1) * P], ident[:, :])
                    last.then_inc(s_htr, 1)

                x_in_array(0)
                tiles(pe, tile)
                down(TILES - 1)

        s_x2in = [sem(f"s_x2in{n}") for n in range(4)]
        s_back = [sem(f"s_back{n}") for n in range(G)]
        s_sum = sem("s_sum")
        s_out = sem("s_out")

        with nc.Block() as block:

            @block.gpsimd
            def _(eng):
                for g in range(G):
                    nc.gpsimd.indirect_dma_start(
                        out=y_all[:, g, :], out_offset=None, in_=sorted_y[:, :],
                        in_offset=bass.IndirectOffsetOnAxis(ap=pos[:, g:g + 1], axis=0)).then_inc(s_back[g], 16)

            @block.sync
            def _(eng):
                q = G // 4
                for n in range(4):
                    eng.dma_start(x2_all[:, n * q:(n + 1) * q, :],
                                  x2_dram[n * q:(n + 1) * q, :, :].rearrange("g p n -> p g n")).then_inc(s_x2in[n], 16)
                for g in range(G):
                    eng.wait_ge(s_sum, g + 1)
                    eng.dma_start(out[g, :, :], y_all[:, g, :]).then_inc(s_out, 16)
                eng.wait_ge(s_out, 16 * G)

            @block.vector
            def _(dve):
                for g in range(G):
                    if g % (G // 4) == 0:
                        dve.wait_ge(s_x2in[g // (G // 4)], 16)
                    dve.wait_ge(s_back[g], 16)
                    nc.vector.tensor_tensor(y_all[:, g, :], y_all[:, g, :], x2_all[:, g, :], ALU.add)\
                        .then_inc(s_sum, 1)


_NAMES = {
    "x_rows": "x", "ctx_cols": "ctx_2048", "skip": "fside_S2_0", "g_xattn": "g_xattn", "g_ffn": "g_ffn",
    "k": "L0_xattn_k", "router_w": "L0_ffn_router_w", "gate_w": "L0_ffn_gate_w", "up_w": "L0_ffn_up_w",
    "down_w": "L0_ffn_down_w",
}


def kernel(**inputs):
    import numpy as np
    import concourse.bacc as bacc
    from concourse import mybir as mb
    from concourse.bass_utils import run_bass_kernel_spmd

    nb, d, length = inputs["x"].shape
    groups = d // 16

    def by_group(a):
        a = np.asarray(a).reshape(nb, groups, 16, length).transpose(1, 0, 2, 3)
        return a.reshape(groups, nb * 16, length)

    arrays = {n: np.asarray(inputs[m]) for n, m in _NAMES.items()}
    arrays["x_rows"] = by_group(inputs["x"])
    cols = by_group(inputs["ctx_2048"]).reshape(groups, nb * 16, length // 128, 128)
    arrays["ctx_cols"] = cols.transpose(0, 3, 2, 1).reshape(groups, 128, length // 128 * nb * 16)
    nc = bacc.Bacc("TRN2", target_bir_lowering=False, num_devices=1)
    args = []
    for name, a in arrays.items():
        arrays[name] = a = np.ascontiguousarray(a)
        args.append(nc.dram_tensor(name, a.shape, mb.dt.from_np(a.dtype), kind="ExternalInput").ap())
    args.append(nc.dram_tensor("out", arrays["x_rows"].shape, mb.dt.float32, kind="ExternalOutput").ap())
    flamingo_layer_kernel(nc, *args)
    got = run_bass_kernel_spmd(nc, [arrays], core_ids=[0]).results[0]["out"]
    return got.reshape(groups, nb, 16, length).transpose(1, 0, 2, 3).reshape(nb, d, length)
```

```python
import concourse.bass as bass
from concourse import mybir
from contextlib import ExitStack


def flamingo_layer_kernel(
    nc: bass.Bass,
    x_rows: bass.AP,
    ctx_cols: bass.AP,
    skip: bass.AP,
    g_xattn: bass.AP,
    g_ffn: bass.AP,
    k: bass.AP,
    router_w: bass.AP,
    gate_w: bass.AP,
    up_w: bass.AP,
    down_w: bass.AP,
    out: bass.AP,
):
    f32 = mybir.dt.float32
    f32r = mybir.dt.float32r
    i32 = mybir.dt.int32
    ALU = mybir.AluOpType
    ACT = mybir.ActivationFunctionType
    AX = mybir.AxisListType.X

    P = 128
    G, _, L = x_rows.shape
    H = k.shape[0]
    J = 8
    NB = P // (2 * J)
    LB = L // P
    COL = NB * J * J
    E, _, I = gate_w.shape
    IB = I // P
    TILES = G + E - 1
    EPS = 1e-5
    NOBODY = 2 * G * P
    KPAD = P + L
    CH = 4
    CW = LB * I // CH
    MW = CH * CW

    kpad = nc.dram_tensor("kpad", [H, KPAD], f32)
    strips = nc.dram_tensor("strips", [H, P, L], f32)
    x2_dram = nc.dram_tensor("x2_dram", [G, P, L], f32)
    xn2_dram = nc.dram_tensor("xn2_dram", [G, P, L], f32)
    sorted_x = nc.dram_tensor("sorted_x", [(TILES + 2) * P, L + 1], f32)

    base = (nc.sbuf_base + 31) // 32 * 32
    place = [base]

    def put(name, shape, dt=f32, at=None):
        size = 4
        for n in shape[1:]:
            size *= n
        size = (size + 31) // 32 * 32
        if at is None:
            at = place
        t = nc.alloc_sbuf_tensor_at(name, shape, dt, offset=at[0])
        at[0] += size
        return t

    ident = put("ident", [P, P])
    ones = put("ones", [P, P])
    upper = put("upper", [P, P])
    e_minus = put("e_minus", [P, E])
    iota_e = put("iota_e", [P, E])
    bounds = put("bounds", [P, G])
    iota_t = put("iota_t", [P, TILES])
    tanh_x = put("tanh_x", [P, 1])
    tanh_f = put("tanh_f", [P, 1])
    logits = put("logits", [P, G, E])
    pos = put("pos", [P, G], i32)
    tile_q = put("tile_q", [1, TILES], i32)
    load_e = put("load_e", [1, E], i32)
    end_q = put("end_q", [1, E], i32)
    mark_pool = put("mark_pool", [P, 3])
    mark_dve = put("mark_dve", [P, 1])
    n_used = put("n_used", [1, 2], i32)
    stats = put("stats", [P, 6])
    mv1 = put("mv1", [P, 2])
    ve1 = put("ve1", [P, 1])
    sd1 = put("sd1", [P, 1])
    rs1 = put("rs1", [P, 1])
    mv2 = put("mv2", [P, 2])
    ve2 = put("ve2", [P, 1])
    sd2 = put("sd2", [P, 1])
    rs2 = put("rs2", [P, 1])
    raw = put("raw", [P, CH, CW])
    gate_at = place[0]
    gate = put("gate", [P, 4 * MW], f32r)
    place[0] += 4 * G
    up_at = place[0]
    up = put("up", [P, 4 * MW], f32r)
    down_at = place[0]
    down_hi = put("down_hi", [P, MW], f32r)
    down_lo = put("down_lo", [P, MW], f32r)
    ffn_at = place[0]
    xs = put("xs", [P, L + 1])
    xT_raw = put("xT_raw", [P, LB * P])
    xT_hi = put("xT_hi", [P, LB, P], f32r)
    xT_lo = put("xT_lo", [P, LB, P], f32r)
    hid = put("hid", [P, I])
    mid = put("mid", [P, I])
    hT_hi = put("hT_hi", [P, IB, P], f32r)
    hT_lo = put("hT_lo", [P, IB, P], f32r)
    ys = put("ys", [P, L])
    x2s = put("x2s", [P, L])
    id_next = put("id_next", [P, 1])
    id_held = put("id_held", [P, 1])
    id_rows = put("id_rows", [P, 1], i32)

    att = [gate_at]
    kv = put("kv", [P, 2, LB * COL], f32, att)
    kv_hi = put("kv_hi", [P, 2, 2, LB * COL], f32r, att)
    kv_lo = put("kv_lo", [P, 2, 2, LB * COL], f32r, att)
    prod = put("prod", [P, 2, J + 1, LB * P], f32, att)
    t_raw = put("t_raw", [P, 2, L], f32, att)
    t_hi = put("t_hi", [P, 2, 2, L], f32r, att)
    t_lo = put("t_lo", [P, 2, 2, L], f32r, att)
    x_in = put("x_in", [P, 2, L], f32, att)
    x_res = put("x_res", [P, 2, L], f32, att)
    xn = put("xn", [P, L], f32, att)
    xn2 = put("xn2", [P, L], f32, att)
    xn2T = put("xn2T", [P, LB, P], f32, att)
    vT = put("vT", [P, 2, LB * P], f32, att)
    cT = put("cT", [P, 2, LB * P], f32, att)
    cK = put("cK", [P, 2, LB * P], f32, att)
    vc = put("vc", [P, LB * P], f32, att)
    skip_b = put("skip_b", [P, G * 2 * J], f32, att)
    skip_w = put("skip_w", [P, LB * NB, 2], f32, att)
    router = put("router", [P, LB, E], f32, att)
    fill = put("fill", [P, L + 1], f32, att)

    rt = [ffn_at]
    xn_all = put("xn_all", [P, G, L + 1], f32, [gate_at + 2 * MW * 4])
    best = put("best", [P, G], f32, rt)
    hot = put("hot", [P, G, E], f32, rt)
    cand = put("cand", [P, G, E], f32, rt)
    pick = put("pick", [P, G], f32, rt)
    scan_a = put("scan_a", [P, G, E], f32, rt)
    scan_b = put("scan_b", [P, G, E], f32, rt)
    total = put("total", [P, G, E], f32, rt)
    over = put("over", [P, E, G], f32, rt)
    n_tiles = put("n_tiles", [P, E], f32, rt)
    ends = [put(f"ends{n}", [P, E], f32, rt) for n in range(4)]
    used = put("used", [P, E], f32, rt)
    ranks = [put(f"ranks{n}", [P, E], f32, rt) for n in range(4)]
    base_e = put("base_e", [P, E], f32, rt)
    pos_f = put("pos_f", [P, G], f32, rt)
    match = put("match", [P, E, E], f32, rt)
    match2 = put("match2", [P, E, E], f32, rt)
    sel_e = put("sel_e", [P, E], f32, rt)
    sel_end = put("sel_end", [P, E], f32, rt)
    last_q = put("last_q", [P, E], f32, rt)
    past = put("past", [P, TILES, E], f32, rt)
    tq_f = put("tq_f", [P, TILES], f32, rt)

    ctx = ExitStack()
    with ctx:
        def sem(name):
            return ctx.enter_context(nc.semaphore(name))

        psum = [ctx.enter_context(nc.psum_tensor(f"bank{n}", [P, 512], f32)) for n in range(4)]
        pairs = [ctx.enter_context(nc.psum_tensor(f"pair{n}", [P, 1024], f32)) for n in range(2)]

        y_bank = psum
        v_bank = pairs[0][:, 0:512]
        att_bank = pairs[0][:, 512:1024]
        x2T_bank = pairs[1][:, 0:512]
        log_bank = pairs[1][:, 512:512 + E]

        s_const = sem("s_const")
        s_kzero = sem("s_kzero")
        s_kcopy = sem("s_kcopy")
        s_strip = [sem(f"s_strip{n}") for n in range(4)]
        s_zfill = sem("s_zfill")
        s_small = sem("s_small")
        s_tanh = sem("s_tanh")
        s_x = [sem(f"s_x{n}") for n in range(2)]
        s_c = [sem(f"s_c{n}") for n in range(2)]
        s_cK = [sem(f"s_cK{n}") for n in range(2)]
        s_r = [sem(f"s_r{n}") for n in range(2)]
        s_t = sem("s_t")
        s_x2st = [sem(f"s_x2st{n}") for n in range(2)]
        s_xnst = sem("s_xnst")
        s_wraw = [sem(f"s_wraw{n}") for n in range(CH)]
        s_whi = sem("s_whi")
        s_var1 = sem("s_var1")
        s_sd1 = sem("s_sd1")
        s_xn = sem("s_xn")
        s_vtr = sem("s_vtr")
        s_vT = sem("s_vT")
        s_thi = sem("s_thi")
        s_tlo = sem("s_tlo")
        s_kv = sem("s_kv")
        s_khi = sem("s_khi")
        s_klo = sem("s_klo")
        s_skip = sem("s_skip")
        s_skv = sem("s_skv")
        s_skw = sem("s_skw")
        s_skp = sem("s_skp")
        s_y = sem("s_y")
        s_p = sem("s_p")
        s_add = sem("s_add")
        s_att = sem("s_att")
        s_x2 = sem("s_x2")
        s_var2 = sem("s_var2")
        s_sd2 = sem("s_sd2")
        s_xn2 = sem("s_xn2")
        s_x2tr = sem("s_x2tr")
        s_xn2T = sem("s_xn2T")
        s_log = sem("s_log")
        s_logc = sem("s_logc")
        s_ln1 = sem("s_ln1")
        s_ln2 = sem("s_ln2")

        def wait(eng, s, value):
            if isinstance(value, int) and value <= 0:
                return
            eng.wait_ge(s, value)

        def stages(eng, body):
            body(0, 0, 0)
            body(1, 1, 0)
            with eng.Fori(1, G // 2 - 1) as pair:
                body(2 * pair, 0, pair)
                body(2 * pair + 1, 1, pair)
            body(G - 2, 0, G // 2 - 1)
            body(G - 1, 1, G // 2 - 1)

        def blk(g, size=1):
            if isinstance(g, int):
                return slice(g * size, (g + 1) * size)
            return bass.ds(g * size, size)

        def known(g, test):
            return test(g) if isinstance(g, int) else True

        s_ready = [sem(f"s_ready_{n}") for n in ("gate", "up", "down")]

        def weight_chunk(kind, e, c):
            if kind < 2:
                w = gate_w if kind == 0 else up_w
                return w[blk(e), c * P:(c + 1) * P, :].rearrange("o p n -> (o p) n")
            rows = down_w[blk(e), 2 * c * P:(2 * c + 2) * P, :]
            return rows.rearrange("o (k p) n -> p (o k) n", p=P)

        def raw_chunk(kind, c):
            return raw[:, c, :] if kind < 2 else raw[:, c, :].rearrange("p (k n) -> p k n", k=2)

        GATE, UP, DOWN = range(3)

        def load_matrix(eng, kind, e, before=None, q_before=0):
            for c in range(CH):
                if before is not None:
                    eng.wait_ge(s_ready[before], q_before * CH + (c + 1))
                eng.dma_start(raw_chunk(kind, c), weight_chunk(kind, e, c)).then_inc(s_wraw[c], 16)


        def slot_parts(kind, slot, c):
            if kind == 2:
                return down_hi[:, c * CW:(c + 1) * CW], down_lo[:, c * CW:(c + 1) * CW]
            w = gate if kind == 0 else up
            o = slot * 2 * MW + c * CW
            return w[:, o:o + CW], w[:, o + MW:o + MW + CW]

        with nc.Block() as block:

            @block.sync
            def _(eng):
                def rows(dram, g):
                    return dram[blk(g), :, :].rearrange("o p n -> (o p) n")

                def load_x(g, u, n):
                    wait(eng, s_xn, g - 1)
                    eng.dma_start(x_in[:, u, :], rows(x_rows, g)).then_inc(s_x[u], 16)

                def load_cK(g, u):
                    wait(eng, s_kv, 2 * (g - 1))
                    wait(eng, s_skip, g - 1)
                    eng.dma_start(cK[:, u, :], rows(ctx_cols, g)).then_inc(s_cK[u], 16)

                def load_cT(g, u):
                    wait(eng, s_p, (g - 1) * 2 * LB)
                    wait(eng, s_skp, g - 1)
                    eng.dma_start(cT[:, u, :], rows(ctx_cols, g)).then_inc(s_c[u], 16)

                def strip_of(g):
                    return bass.AP(kpad, 2 * g * KPAD + P, [[KPAD, 2], [-1, P], [1, L]])

                STRIP_PARTS = [range(1), range(1, 2), range(2, G // 2), range(G // 2, G)]

                def make_strips(part):
                    for a in STRIP_PARTS[part]:
                        eng.dma_start(strips[2 * a:2 * a + 2, :, :], strip_of(a)).then_inc(s_strip[part], 16)

                def load_t(g):
                    wait(eng, s_thi, g)
                    wait(eng, s_tlo, g)
                    part = 3 if not isinstance(g, int) or g >= G // 2 else min(g, 2)
                    eng.wait_ge(s_strip[part], 16 * len(STRIP_PARTS[part]))
                    eng.dma_start(t_raw[:, :, :], strips[blk(g, 2), :, :].rearrange("h p n -> p h n"))\
                       .then_inc(s_t, 16)

                def store_x2(g, u):
                    eng.wait_ge(s_x2, g + 1)
                    eng.dma_start(rows(x2_dram, g), x_res[:, u, :]).then_inc(s_x2st[u], 16)

                def store_xn2(g):
                    eng.wait_ge(s_xn2, g + 1)
                    eng.dma_start(rows(xn2_dram, g), xn2[:, :]).then_inc(s_xnst, 16)

                def stage(g, u, n):
                    if known(g, lambda g: g < G - 2):
                        load_x(g + 2, u, n)
                    if known(g, lambda g: g < G - 1):
                        load_cK(g + 1, 1 - u)
                    load_cT(g, u)
                    if known(g, lambda g: g < G - 1):
                        load_t(g + 1)
                    if known(g, lambda g: g >= 2):
                        store_x2(g - 2, u)
                        store_xn2(g - 2)
                        eng.wait_ge(s_x2st[u], 16 * n)
                    eng.dma_start(x_res[:, u, :], rows(x_rows, g)).then_inc(s_r[u], 16)
                    if isinstance(g, int) and g < 2:
                        make_strips(2 + g)
                    if isinstance(g, int) and g == G - 2:
                        eng.wait_ge(s_const, 2)
                        load_matrix(eng, GATE, 0)
                        for t in range(TILES + 2):
                            eng.dma_start(sorted_x[t * P:(t + 1) * P, :], fill[:, :]).then_inc(s_zfill, 16)

                eng.dma_start(kpad[:, P:KPAD], k).then_inc(s_kcopy, 16)
                load_x(0, 0, 0)
                eng.wait_ge(s_const, 1)
                eng.dma_start(kpad[:, 0:P], fill[0:H, 0:P]).then_inc(s_kzero, 16)
                load_x(1, 1, 0)
                load_cK(0, 0)
                eng.wait_ge(s_kcopy, 16)
                eng.wait_ge(s_kzero, 16)
                make_strips(0)
                load_t(0)
                eng.dma_start(tanh_x[:, :], bass.AP(g_xattn.tensor, 0, [[0, P], [1, 1]])).then_inc(s_small, 16)
                eng.dma_start(tanh_f[:, :], bass.AP(g_ffn.tensor, 0, [[0, P], [1, 1]])).then_inc(s_small, 16)
                eng.dma_start(skip_b[:, :], bass.AP(skip.tensor, 0, [[0, P], [1, G * 2 * J]])).then_inc(s_small, 16)
                eng.dma_start(router[:, :, :], router_w.rearrange("(b p) e -> p b e", p=P)).then_inc(s_small, 16)
                make_strips(1)
                stages(eng, stage)
                for g in (G - 2, G - 1):
                    store_x2(g, g % 2)
                    store_xn2(g)
                for u in range(2):
                    eng.wait_ge(s_x2st[u], 16 * (G // 2))
                eng.wait_ge(s_xnst, 16 * G)
                eng.wait_ge(s_zfill, 16 * (TILES + 2))

            @block.gpsimd
            def _(eng):
                nc.gpsimd.memset(fill[:, 0:L], 0.0).then_inc(s_const, 1)
                nc.gpsimd.memset(fill[:, L:L + 1], float(NOBODY)).then_inc(s_const, 1)
                nc.gpsimd.memset(ident[:, :], 0.0).then_inc(s_const, 1)
                nc.gpsimd.memset(ones[:, :], 1.0).then_inc(s_const, 1)
                eng.wait_ge(s_const, 4)
                nc.gpsimd.affine_select(out=ident[:, :], in_=ident[:, :], compare_op=ALU.not_equal, fill=1.0,
                                        base=0, pattern=[[-1, P]], channel_multiplier=1).then_inc(s_const, 1)
                nc.gpsimd.affine_select(out=upper[:, :], in_=ones[:, :], compare_op=ALU.is_gt, fill=0.0,
                                        base=0, pattern=[[1, P]], channel_multiplier=-1).then_inc(s_const, 1)
                for t, base0, step in ((e_minus, 1 - E, 1), (iota_e, 0, 1), (bounds, 0, P), (iota_t, 0, 1)):
                    nc.gpsimd.iota(t[:, :], pattern=[[step, t.shape[1]]], base=base0, channel_multiplier=0,
                                   allow_small_or_imprecise_dtypes=True).then_inc(s_const, 1)

                def outer(g, u, n, hh):
                    h = 2 * g + hh
                    if hh == 0:
                        eng.wait_ge(s_vT, g + 1)
                        eng.wait_ge(s_cK[u], 16 * (n + 1))
                    wait(eng, s_khi, h - 1)
                    wait(eng, s_klo, h - 1)
                    v = vT[:, u, :].rearrange("p (a r) -> p a r", r=2 * J)[:, :, hh * J:(hh + 1) * J]
                    c = cK[:, u, :].rearrange("p (a r) -> p a r", r=2 * J)[:, :, hh * J:(hh + 1) * J]
                    nc.gpsimd.tensor_tensor(
                        kv[:, hh, :].rearrange("p (a i j) -> p a i j", i=J, j=J),
                        v.unsqueeze(3).broadcast_to([P, LB * NB, J, J]),
                        c.unsqueeze(2).broadcast_to([P, LB * NB, J, J]), ALU.mult).then_inc(s_kv, 1)

                def skip_first(g, u):
                    a = LB * NB
                    wait(eng, s_skw, g)
                    wait(eng, s_skip, g)
                    s_g = skip_b[:, blk(g, 2 * J)]
                    nc.gpsimd.tensor_tensor(
                        vc[:, :].rearrange("p (a r) -> p a r", r=2 * J),
                        vT[:, u, :].rearrange("p (a r) -> p a r", r=2 * J),
                        s_g.unsqueeze(1).broadcast_to([P, a, 2 * J]), ALU.mult).then_inc(s_skv, 1)
                    eng.wait_ge(s_skv, g + 1)
                    nc.gpsimd.tensor_tensor(vc[:, :], vc[:, :], cK[:, u, :], ALU.mult).then_inc(s_skip, 1)

                def skip_last(g, u, n):
                    eng.wait_ge(s_skw, g + 1)
                    eng.wait_ge(s_c[u], 16 * (n + 1))
                    wait(eng, s_att, g - 1)
                    nc.gpsimd.tensor_tensor(
                        prod[:, u, J, :].rearrange("p (a h j) -> p a h j", h=2, j=J),
                        cT[:, u, :].rearrange("p (a h j) -> p a h j", h=2, j=J),
                        skip_w[:, :, :].unsqueeze(3).broadcast_to([P, LB * NB, 2, J]), ALU.mult)\
                        .then_inc(s_skp, 1)

                def add_pairs(g, u, hh):
                    eng.wait_ge(s_p, (2 * g + hh + 1) * LB)
                    terms = prod[:, u, 0:J, :].rearrange("p i (a r) -> p i a r", r=2 * J)[:, :, :, hh * J:(hh + 1) * J]
                    nc.gpsimd.tensor_tensor(terms[:, 0:J // 2], terms[:, 0:J // 2], terms[:, J // 2:J], ALU.add)\
                        .then_inc(s_add, 1)

                def before_conv(g, u, n):
                    outer(g, u, n, 0)
                    if isinstance(g, int) and g == 0:
                        eng.wait_ge(s_small, 64)
                    skip_first(g, u)
                    outer(g, u, n, 1)

                def stage(g, u, n):
                    if known(g, lambda g: g >= 1):
                        add_pairs(g - 1, 1 - u, 1)
                    skip_last(g, u, n)
                    if known(g, lambda g: g < G - 1):
                        before_conv(g + 1, 1 - u, n + u)
                    add_pairs(g, u, 0)

                before_conv(0, 0, 0)
                stages(eng, stage)
                add_pairs(G - 1, 1, 1)

            @block.scalar
            def _(act):
                def root1(g):
                    act.wait_ge(s_var1, g + 1)
                    nc.scalar.activation(sd1[:, :], ve1[:, :], ACT.Sqrt).then_inc(s_sd1, 1)

                def strip_hi(g, u):
                    act.wait_ge(s_t, 16 * (g + 1))
                    wait(act, s_y, (g - 1) * 2 * LB)
                    nc.scalar.activation(t_hi[:, u, :, :], t_raw[:, :, :], ACT.Copy).then_inc(s_thi, 1)

                def v_out(g, u):
                    act.wait_ge(s_vtr, g + 1)
                    wait(act, s_kv, 2 * (g - 1))
                    wait(act, s_skip, g - 1)
                    nc.scalar.activation(vT[:, u, :], v_bank, ACT.Copy).then_inc(s_vT, 1)

                def kv_high(g, u, hh):
                    h = 2 * g + hh
                    act.wait_ge(s_kv, h + 1)
                    wait(act, s_y, (h - 3) * LB)
                    nc.scalar.activation(kv_hi[:, u, hh, :], kv[:, hh, :], ACT.Copy).then_inc(s_khi, 1)

                def logits_out(g):
                    act.wait_ge(s_log, g + 1)
                    nc.scalar.activation(logits[:, blk(g), :].rearrange("p o e -> p (o e)"), log_bank, ACT.Copy)\
                        .then_inc(s_logc, 1)

                def root2(g):
                    act.wait_ge(s_var2, g + 1)
                    nc.scalar.activation(sd2[:, :], ve2[:, :], ACT.Sqrt).then_inc(s_sd2, 1)

                def xn2T_out(g):
                    act.wait_ge(s_x2tr, g + 1)
                    wait(act, s_log, g)
                    nc.scalar.activation(xn2T[:, :, :].rearrange("p b t -> p (b t)"), x2T_bank, ACT.Copy)\
                        .then_inc(s_xn2T, 1)

                def stage(g, u, n):
                    more = known(g, lambda g: g < G - 1)
                    before = known(g, lambda g: g >= 1)
                    if known(g, lambda g: g < G - 2):
                        root1(g + 2)
                    if more:
                        kv_high(g + 1, 1 - u, 0)
                    if known(g, lambda g: g >= 2):
                        logits_out(g - 2)
                    if before:
                        root2(g - 1)
                    if more:
                        strip_hi(g + 1, 1 - u)
                        kv_high(g + 1, 1 - u, 1)
                    if known(g, lambda g: g < G - 2):
                        v_out(g + 2, u)
                    if before:
                        xn2T_out(g - 1)

                root1(0)
                v_out(0, 0)
                root1(1)
                v_out(1, 1)
                strip_hi(0, 0)
                kv_high(0, 0, 0)
                act.wait_ge(s_small, 64)
                nc.scalar.activation(tanh_x[:, :], tanh_x[:, :], ACT.Tanh).then_inc(s_tanh, 1)
                nc.scalar.activation(tanh_f[:, :], tanh_f[:, :], ACT.Tanh).then_inc(s_tanh, 1)
                kv_high(0, 0, 1)
                stages(act, stage)
                logits_out(G - 2)
                root2(G - 1)
                xn2T_out(G - 1)
                logits_out(G - 1)

            @block.vector
            def _(dve):
                def norm_first(src, mv, ve, done, steps, g):
                    nc.vector.bn_stats(stats[:, :], src).then_inc(steps, 1)
                    dve.wait_ge(steps, 3 * g + 1)
                    nc.vector.tensor_copy(mark_dve[:, :], stats[:, 0:1])
                    nc.vector.bn_aggr(mv[:, :], stats[:, :]).then_inc(steps, 1)
                    dve.wait_ge(steps, 3 * g + 2)
                    nc.vector.tensor_scalar(ve[:, :], mv[:, 1:2], EPS, None, ALU.add).then_inc(done, 1)

                def norm_last(dst, src, mv, sd, rs, s_sd, done, steps, g):
                    dve.wait_ge(s_sd, g + 1)
                    nc.vector.reciprocal(rs[:, :], sd[:, :]).then_inc(steps, 1)
                    dve.wait_ge(steps, 3 * g + 3)
                    nc.vector.tensor_scalar(dst, src, mv[:, 0:1], rs[:, 0:1], ALU.subtract, ALU.mult)\
                        .then_inc(done, 1)

                def ln1(g, u, n):
                    dve.wait_ge(s_x[u], 16 * (n + 1))
                    norm_first(x_in[:, u, :], mv1, ve1, s_var1, s_ln1, g)
                    wait(dve, s_vtr, g)
                    norm_last(xn[:, :], x_in[:, u, :], mv1, sd1, rs1, s_sd1, s_xn, s_ln1, g)

                def strip_lo(g, u):
                    dve.wait_ge(s_thi, g + 1)
                    wait(dve, s_y, (g - 1) * 2 * LB)
                    nc.vector.tensor_tensor(t_lo[:, u, :, :], t_raw[:, :, :], t_hi[:, u, :, :].bitcast(f32),
                                            ALU.subtract).then_inc(s_tlo, 1)

                def kv_low(g, u, hh):
                    h = 2 * g + hh
                    dve.wait_ge(s_khi, h + 1)
                    wait(dve, s_y, (h - 3) * LB)
                    nc.vector.tensor_tensor(kv_lo[:, u, hh, :], kv[:, hh, :], kv_hi[:, u, hh, :].bitcast(f32),
                                            ALU.subtract).then_inc(s_klo, 1)

                def product(g, u, n, hh, lb):
                    h = 2 * g + hh
                    if hh == 0 and lb == 0:
                        dve.wait_ge(s_c[u], 16 * (n + 1))
                        wait(dve, s_att, g - 1)
                    dve.wait_ge(s_y, h * LB + lb + 1)
                    c = cT[:, u, lb * P:(lb + 1) * P].rearrange("p (b r) -> p b r", r=2 * J)
                    c = c[:, :, hh * J:(hh + 1) * J].unsqueeze(3).broadcast_to([P, NB, J, J])
                    dst = prod[:, u, 0:J, lb * P:(lb + 1) * P].rearrange("p i (b r) -> p b i r", r=2 * J)
                    nc.vector.tensor_tensor(dst[:, :, :, hh * J:(hh + 1) * J],
                                            y_bank[lb][:, :].rearrange("p (b i j) -> p b i j", i=J, j=J),
                                            c, ALU.mult).then_inc(s_p, 1)

                def residual(g, u, n):
                    dve.wait_ge(s_att, g + 1)
                    dve.wait_ge(s_r[u], 16 * (n + 1))
                    nc.vector.scalar_tensor_tensor(out=x_res[:, u, :], in0=att_bank, scalar=tanh_x[:, 0:1],
                                                   in1=x_res[:, u, :], op0=ALU.mult, op1=ALU.add)\
                        .then_inc(s_x2, 1)

                def ln2_first(g, u):
                    dve.wait_ge(s_x2, g + 1)
                    norm_first(x_res[:, u, :], mv2, ve2, s_var2, s_ln2, g)

                def ln2_last(g, u):
                    wait(dve, s_x2tr, g)
                    wait(dve, s_xnst, 16 * g)
                    norm_last(xn2[:, :], x_res[:, u, :], mv2, sd2, rs2, s_sd2, s_xn2, s_ln2, g)

                def skip_sum(g):
                    dve.wait_ge(s_skip, g + 1)
                    wait(dve, s_skp, g)
                    nc.vector.tensor_reduce(skip_w[:, :, :],
                                            vc[:, :].rearrange("p (a h i) -> p a h i", h=2, i=J), AX, ALU.add)\
                        .then_inc(s_skw, 1)

                def stage(g, u, n):
                    more = known(g, lambda g: g < G - 1)
                    before = known(g, lambda g: g >= 1)
                    product(g, u, n, 0, 0)
                    product(g, u, n, 0, 1)
                    if known(g, lambda g: g < G - 2):
                        ln1(g + 2, u, n + 1)
                    product(g, u, n, 0, 2)
                    if before:
                        residual(g - 1, 1 - u, n - 1 + u)
                        ln2_first(g - 1, 1 - u)
                    product(g, u, n, 0, 3)
                    if before:
                        ln2_last(g - 1, 1 - u)
                    if more:
                        kv_low(g + 1, 1 - u, 0)
                        strip_lo(g + 1, 1 - u)
                    product(g, u, n, 1, 0)
                    product(g, u, n, 1, 1)
                    if more:
                        skip_sum(g + 1)
                    product(g, u, n, 1, 2)
                    product(g, u, n, 1, 3)
                    if more:
                        kv_low(g + 1, 1 - u, 1)

                ln1(0, 0, 0)
                ln1(1, 1, 0)
                strip_lo(0, 0)
                kv_low(0, 0, 0)
                skip_sum(0)
                kv_low(0, 0, 1)
                dve.wait_ge(s_tanh, 2)
                stages(dve, stage)
                residual(G - 1, 1, G // 2 - 1)
                ln2_first(G - 1, 1)
                ln2_last(G - 1, 1)

            @block.tensor
            def _(pe):
                def transposes(bank, src, done):
                    for b in range(LB):
                        last = nc.tensor.transpose(bank[:, b * P:(b + 1) * P], src[:, b * P:(b + 1) * P],
                                                   ident[:, :])
                    last.then_inc(done, 1)

                def v_in(g):
                    pe.wait_ge(s_xn, g + 1)
                    wait(pe, s_vT, g)
                    transposes(v_bank, xn, s_vtr)

                def conv(g, u, hh, blocks):
                    h = 2 * g + hh
                    for lb in blocks:
                        if lb == 0:
                            pe.wait_ge(s_klo, h + 1)
                            if hh == 0:
                                pe.wait_ge(s_tlo, g + 1)
                        wait(pe, s_p, (h - 1) * LB + lb + 1)
                        for mb in range(lb + 1):
                            d = lb - mb
                            for n, (t, v) in enumerate(((t_hi, kv_hi), (t_hi, kv_lo), (t_lo, kv_hi))):
                                last = nc.tensor.matmul(
                                    y_bank[lb][:, :], t[:, u, hh, d * P:(d + 1) * P],
                                    v[:, u, hh, mb * COL:(mb + 1) * COL],
                                    start=(mb == 0 and n == 0), stop=(mb == lb and n == 2))
                        last.then_inc(s_y, 1)

                def logits_of(g):
                    pe.wait_ge(s_xn2T, g + 1)
                    wait(pe, s_logc, g)
                    for b in range(LB):
                        last = nc.tensor.matmul(log_bank, xn2T[:, b, :], router[:, b, :],
                                                start=(b == 0), stop=(b == LB - 1))
                    last.then_inc(s_log, 1)

                def sum_heads(g, u):
                    pe.wait_ge(s_add, 2 * (g + 1))
                    pe.wait_ge(s_skp, g + 1)
                    wait(pe, s_x2, g)
                    terms = [*range(J // 2), J]
                    for lb in range(LB):
                        for i in terms:
                            last = nc.tensor.matmul(att_bank[:, lb * P:(lb + 1) * P],
                                                    prod[:, u, i, lb * P:(lb + 1) * P], ident[:, :],
                                                    start=(i == 0), stop=(i == J), is_transpose=True)
                    last.then_inc(s_att, 1)

                def x2_in(g):
                    pe.wait_ge(s_xn2, g + 1)
                    wait(pe, s_xn2T, g)
                    transposes(x2T_bank, xn2, s_x2tr)

                def stage(g, u, n):
                    before = known(g, lambda g: g >= 1)
                    conv(g, u, 0, (0, 1, 2))
                    if known(g, lambda g: g >= 2):
                        logits_of(g - 2)
                    if before:
                        sum_heads(g - 1, 1 - u)
                    conv(g, u, 0, (3,))
                    conv(g, u, 1, (0, 1, 2))
                    if known(g, lambda g: g < G - 2):
                        v_in(g + 2)
                    if before:
                        x2_in(g - 1)
                    conv(g, u, 1, (3,))

                pe.wait_ge(s_const, 6)
                v_in(0)
                v_in(1)
                stages(pe, stage)
                logits_of(G - 2)
                sum_heads(G - 1, 1)
                x2_in(G - 1)
                logits_of(G - 1)

        s_xall = [sem(f"s_xall{n}") for n in range(4)]
        s_hot = sem("s_hot")
        s_cnt = sem("s_cnt")
        s_pos = sem("s_pos")
        s_tab = sem("s_tab")
        s_num = sem("s_num")
        s_scat = [sem(f"s_scat{n}") for n in range(G)]
        s_rt = sem("s_rt")

        with nc.Block() as block:

            @block.sync
            def _(eng):
                for n in range(4):
                    q = G // 4
                    eng.dma_start(xn_all[:, n * q:(n + 1) * q, 0:L],
                                  xn2_dram[n * q:(n + 1) * q, :, :].rearrange("g p n -> p g n")).then_inc(s_xall[n], 16)
                load_matrix(eng, UP, 0, GATE, 0)
                load_matrix(eng, DOWN, 0, UP, 0)

            @block.scalar
            def _(act):
                for kind in (GATE, UP):
                    for c in range(CH):
                        act.wait_ge(s_wraw[c], 16 * (kind + 1))
                        nc.scalar.activation(slot_parts(kind, 0, c)[0], raw[:, c, :], ACT.Copy).then_inc(s_whi, 1)

            @block.tensor
            def _(pe):
                pe.wait_ge(s_hot, 1)
                flat = hot[:, :, :].rearrange("p g e -> p (g e)")
                nc.tensor.matmul(psum[0][:, 0:G * E], upper[:, :], flat, start=True, stop=True)
                nc.tensor.matmul(psum[1][:, 0:G * E], ones[:, :], flat, start=True, stop=True).then_inc(s_cnt, 1)

            @block.vector
            def _(dve):
                done = [0]

                def step(instruction):
                    done[0] += 1
                    instruction.then_inc(s_rt, 1)
                    dve.wait_ge(s_rt, done[0])

                V = nc.vector
                ge = [P, G, E]
                step(V.tensor_reduce(best[:, :], logits[:, :, :], AX, ALU.max))
                step(V.tensor_tensor(cand[:, :, :], logits[:, :, :], best[:, :].unsqueeze(2).broadcast_to(ge),
                                     ALU.is_equal))
                step(V.tensor_tensor(hot[:, :, :], cand[:, :, :], e_minus[:, :].unsqueeze(1).broadcast_to(ge),
                                     ALU.mult))
                step(V.tensor_reduce(pick[:, :], hot[:, :, :], AX, ALU.min))
                V.tensor_tensor(hot[:, :, :], e_minus[:, :].unsqueeze(1).broadcast_to(ge),
                                pick[:, :].unsqueeze(2).broadcast_to(ge), ALU.is_equal).then_inc(s_hot, 1)
                dve.wait_ge(s_cnt, 1)
                step(V.tensor_copy(total[:, :, :], psum[1][:, 0:G * E].rearrange("p (g e) -> p g e", e=E)))
                src, dst = total, scan_a
                shift = 1
                while shift < G:
                    V.tensor_copy(dst[:, 0:shift, :], src[:, 0:shift, :])
                    step(V.tensor_tensor(dst[:, shift:G, :], src[:, shift:G, :], src[:, 0:G - shift, :], ALU.add))
                    src, dst = dst, (scan_b if dst is scan_a else scan_a)
                    shift *= 2
                counts = src[:, G - 1, :]
                step(V.tensor_tensor(over[:, :, :], counts.unsqueeze(2).broadcast_to([P, E, G]),
                                     bounds[:, :].unsqueeze(1).broadcast_to([P, E, G]), ALU.is_gt))
                step(V.tensor_reduce(n_tiles[:, :], over[:, :, :], AX, ALU.add))
                step(V.tensor_scalar(n_tiles[:, 0:1], n_tiles[:, 0:1], 1.0, None, ALU.max))
                step(V.tensor_scalar(used[:, :], n_tiles[:, :], 0.0, None, ALU.is_gt))
                step(V.tensor_copy(ends[0][:, :], n_tiles[:, :]))
                step(V.tensor_copy(ranks[0][:, :], used[:, :]))
                for n, shift in enumerate((1, 2, 4)):
                    for s in (ends, ranks):
                        V.tensor_copy(s[n + 1][:, 0:shift], s[n][:, 0:shift])
                        step(V.tensor_tensor(s[n + 1][:, shift:E], s[n][:, shift:E], s[n][:, 0:E - shift], ALU.add))
                end_e, rank_e = ends[3], ranks[3]
                step(V.tensor_tensor(base_e[:, :], end_e[:, :], n_tiles[:, :], ALU.subtract))
                step(V.tensor_scalar(base_e[:, :], base_e[:, :], float(P), None, ALU.mult))
                step(V.tensor_tensor(dst[:, :, :], src[:, :, :], total[:, :, :], ALU.subtract))
                step(V.tensor_tensor(dst[:, :, :], psum[0][:, 0:G * E].rearrange("p (g e) -> p g e", e=E),
                                     dst[:, :, :], ALU.add))
                step(V.tensor_tensor(dst[:, :, :], dst[:, :, :], base_e[:, :].unsqueeze(1).broadcast_to(ge), ALU.add))
                step(V.tensor_tensor(dst[:, :, :], dst[:, :, :], hot[:, :, :], ALU.mult))
                step(V.tensor_reduce(pos_f[:, :], dst[:, :, :], AX, ALU.add))
                V.tensor_copy(pos[:, :], pos_f[:, :]).then_inc(s_pos, 1)
                ee = [P, E, E]
                step(V.tensor_scalar(last_q[:, :], iota_e[:, :], rank_e[:, E - 1:E], -1.0, ALU.subtract, ALU.is_ge))
                step(V.tensor_scalar(last_q[:, :], last_q[:, :], end_e[:, E - 1:E], None, ALU.mult))
                step(V.tensor_scalar(rank_e[:, :], rank_e[:, :], -1.0, None, ALU.add))
                step(V.tensor_tensor(match[:, :, :], rank_e[:, :].unsqueeze(1).broadcast_to(ee),
                                     iota_e[:, :].unsqueeze(2).broadcast_to(ee), ALU.is_equal))
                step(V.tensor_tensor(match[:, :, :], match[:, :, :], used[:, :].unsqueeze(1).broadcast_to(ee),
                                     ALU.mult))
                step(V.tensor_tensor(match2[:, :, :], match[:, :, :], iota_e[:, :].unsqueeze(1).broadcast_to(ee),
                                     ALU.mult))
                step(V.tensor_reduce(sel_e[:, :], match2[:, :, :], AX, ALU.add))
                step(V.tensor_tensor(match2[:, :, :], match[:, :, :], end_e[:, :].unsqueeze(1).broadcast_to(ee),
                                     ALU.mult))
                step(V.tensor_reduce(sel_end[:, :], match2[:, :, :], AX, ALU.add))
                step(V.tensor_tensor(sel_end[:, :], sel_end[:, :], last_q[:, :], ALU.max))
                te = [P, TILES, E]
                step(V.tensor_tensor(past[:, :, :], iota_t[:, :].unsqueeze(2).broadcast_to(te),
                                     sel_end[:, :].unsqueeze(1).broadcast_to(te), ALU.is_ge))
                step(V.tensor_reduce(tq_f[:, :], past[:, :, :], AX, ALU.add))
                V.tensor_copy(load_e[:, :], sel_e[0:1, :])
                V.tensor_copy(end_q[:, :], sel_end[0:1, :])
                V.tensor_copy(n_used[:, 0:1], end_e[0:1, E - 1:E])
                V.tensor_scalar(n_used[:, 1:2], end_e[0:1, E - 1:E], -1.0, None, ALU.add)
                V.tensor_copy(tile_q[:, :], tq_f[0:1, :]).then_inc(s_tab, 1)
                for kind in (GATE, UP):
                    for c in range(CH):
                        hi, lo = slot_parts(kind, 0, c)
                        dve.wait_ge(s_whi, kind * CH + c + 1)
                        V.tensor_tensor(lo, raw[:, c, :], hi.bitcast(f32), ALU.subtract).then_inc(s_ready[kind], 1)

            @block.gpsimd
            def _(eng):
                nc.gpsimd.iota(xn_all[:, :, L:L + 1], pattern=[[P, G]], base=0, channel_multiplier=1,
                               allow_small_or_imprecise_dtypes=True).then_inc(s_num, 1)
                eng.wait_ge(s_num, 1)
                eng.wait_ge(s_pos, 1)
                for g in range(G):
                    if g % (G // 4) == 0:
                        eng.wait_ge(s_xall[g // (G // 4)], 16)
                    nc.gpsimd.indirect_dma_start(
                        out=sorted_x[:, :], out_offset=bass.IndirectOffsetOnAxis(ap=pos[:, g:g + 1], axis=0),
                        in_=xn_all[:, g, :], in_offset=None).then_inc(s_scat[g], 16)
                for g in range(G):
                    eng.wait_ge(s_scat[g], 16)

        gate_bank = pairs[0]
        up_bank = pairs[1]
        x_bank, out_bank = psum[0], psum[1]
        h_bank = psum[2:4]
        s_xs = sem("s_xs")
        s_xtr = sem("s_xtr")
        s_xT = sem("s_xT")
        s_xlo = sem("s_xlo")
        s_gate = sem("s_gate")
        s_up = sem("s_up")
        s_down = sem("s_down")
        s_silu = sem("s_silu")
        s_upc = sem("s_upc")
        s_hid = sem("s_hid")
        s_htr = sem("s_htr")
        s_hT = sem("s_hT")
        s_hlo = sem("s_hlo")
        s_ys = sem("s_ys")
        s_next = sem("s_next")
        s_held = sem("s_held")
        s_ids = sem("s_ids")
        s_clean = sem("s_clean")
        s_x2s = sem("s_x2s")
        s_add = sem("s_add_y")
        s_out = sem("s_out")

        FIRST = 5

        def tiles(eng, body):
            in_use = eng.value_load(n_used[0:1, 0:1], min_val=G, max_val=TILES)
            last = eng.value_load(n_used[0:1, 1:2], min_val=G - 1, max_val=TILES - 1)
            body(0)
            with eng.Fori(1, TILES) as t:
                with eng.If(t < in_use):
                    body(t)
            return last

        def flat(t):
            return t[:, :, :].rearrange("p b t -> p (b t)")

        with nc.Block() as block:

            @block.sync
            def _(eng):
                def expert(q):
                    return eng.value_load(load_e[0:1, blk(q)], min_val=0, max_val=E - 1)

                second_e = expert(1)
                load_matrix(eng, GATE, second_e, DOWN, 0)
                load_matrix(eng, UP, second_e, GATE, 1)

                def load_three(q, before, q_before):
                    ahead = expert(q + 2)
                    load_matrix(eng, GATE, ahead, before, q_before)
                    load_matrix(eng, UP, ahead, GATE, q + 2)
                    load_matrix(eng, DOWN, expert(q + 1), UP, q + 2)

                load_three(0, UP, 1)
                with eng.Fori(1, E - 2) as q:
                    load_three(q, DOWN, q)
                load_matrix(eng, DOWN, expert(E - 1), DOWN, E - 2)

            @block.vector
            def _(dve):
                def split_matrix(kind, slot, count):
                    for c in range(CH):
                        hi, lo = slot_parts(kind, slot, c)
                        dve.wait_ge(s_wraw[c], (count + 1) * 16)
                        nc.vector.tensor_copy(hi, raw[:, c, :]).then_inc(s_whi, 1)
                        dve.wait_ge(s_whi, count * CH + (c + 1))
                        nc.vector.tensor_tensor(lo, raw[:, c, :], hi.bitcast(f32), ALU.subtract)\
                            .then_inc(s_ready[kind], 1)

                split_matrix(DOWN, 0, 2)
                split_matrix(GATE, 1, 3)
                split_matrix(UP, 1, 4)
                with dve.Fori(0, E // 2 - 1) as pair:
                    for u in range(2):
                        q = 2 * pair + u
                        end = dve.value_load(end_q[0:1, blk(q)], min_val=1, max_val=TILES)
                        dve.wait_ge(s_gate, end)
                        split_matrix(GATE, u, 3 * q + FIRST)
                        dve.wait_ge(s_up, end)
                        split_matrix(UP, u, 3 * q + (FIRST + 1))
                        dve.wait_ge(s_down, end)
                        split_matrix(DOWN, 0, 3 * q + (FIRST + 2))
                end = dve.value_load(end_q[0:1, E - 2:E - 1], min_val=1, max_val=TILES)
                dve.wait_ge(s_down, end)
                split_matrix(DOWN, 0, 3 * E - 1)

            @block.scalar
            def _(act):
                def load(t):
                    act.dma_start(xs[:, :], sorted_x[blk(t, P), :]).then_inc(s_xs, 16)

                def x_parts(t):
                    act.wait_ge(s_xtr, t + 1)
                    nc.scalar.activation(flat(xT_hi), x_bank[:, :], ACT.Copy)
                    wait(act, s_xlo, t)
                    nc.scalar.activation(xT_raw[:, :], x_bank[:, :], ACT.Copy).then_inc(s_xT, 1)

                def out_tile(t):
                    act.wait_ge(s_down, t + 1)
                    wait(act, s_out, 16 * t)
                    nc.scalar.activation(ys[:, :], out_bank[:, :], ACT.Copy, scale=tanh_f[:, 0:1]).then_inc(s_ys, 1)

                def tile(t):
                    act.wait_ge(s_gate, t + 1)
                    nc.scalar.activation(hid[:, :], gate_bank[:, :], ACT.Silu).then_inc(s_silu, 1)
                    act.wait_ge(s_up, t + 1)
                    wait(act, s_hlo, t)
                    nc.scalar.activation(mid[:, :], up_bank[:, :], ACT.Copy).then_inc(s_upc, 1)
                    x_parts(t + 1)
                    if known(t, lambda t: t > 0):
                        out_tile(t - 1)
                    act.wait_ge(s_next, t + 2)
                    load(t + 2)
                    act.wait_ge(s_htr, t + 1)
                    act.wait_ge(s_hid, t + 1)
                    for n in range(2):
                        nc.scalar.activation(hT_hi[:, n * LB:(n + 1) * LB, :].rearrange("p b t -> p (b t)"),
                                             h_bank[n][:, :], ACT.Copy)
                    for n in range(2):
                        last = nc.scalar.activation(mid[:, n * 512:(n + 1) * 512], h_bank[n][:, :], ACT.Copy)
                    last.then_inc(s_hT, 1)

                load(0)
                x_parts(0)
                act.wait_ge(s_next, 1)
                load(1)
                last_tile = tiles(act, tile)
                act.wait_ge(s_xs, 16 * last_tile + 48)
                out_tile(last_tile)

            @block.gpsimd
            def _(eng):
                one = ones[:, 0:1]

                def after(place, *waits):
                    for s, value in waits:
                        wait(eng, s, value)
                    nc.gpsimd.tensor_tensor(mark_pool[:, place:place + 1], one, one, ALU.mult)

                def low_x(t):
                    eng.wait_ge(s_xT, t + 1)
                    nc.gpsimd.tensor_tensor(flat(xT_lo), xT_raw[:, :], flat(xT_hi).bitcast(f32), ALU.subtract)\
                        .then_inc(s_xlo, 1)
                    wait(eng, s_held, t)
                    nc.gpsimd.tensor_tensor(id_next[:, :], xs[:, L:L + 1], one, ALU.mult).then_inc(s_next, 1)

                def out_rows(t):
                    eng.wait_ge(s_ys, t + 1)
                    eng.wait_ge(s_x2s, 16 * (t + 1))
                    nc.gpsimd.tensor_tensor(ys[:, :], ys[:, :], x2s[:, :], ALU.add).then_inc(s_add, 1)
                    after(0, (s_add, t + 1))
                    nc.gpsimd.indirect_dma_start(
                        out=out.rearrange("g p n -> (g p) n"),
                        out_offset=bass.IndirectOffsetOnAxis(ap=id_rows[:, 0:1], axis=0),
                        in_=ys[:, :], in_offset=None, bounds_check=G * P - 1, oob_is_err=False).then_inc(s_out, 16)

                def tile(t):
                    eng.wait_ge(s_next, t + 1)
                    nc.gpsimd.tensor_tensor(id_held[:, :], id_next[:, :], one, ALU.mult).then_inc(s_held, 1)
                    eng.wait_ge(s_silu, t + 1)
                    eng.wait_ge(s_upc, t + 1)
                    nc.gpsimd.tensor_tensor(hid[:, :], hid[:, :], mid[:, :], ALU.mult).then_inc(s_hid, 1)
                    low_x(t + 1)
                    if known(t, lambda t: t > 0):
                        out_rows(t - 1)
                    eng.wait_ge(s_hT, t + 1)
                    nc.gpsimd.tensor_tensor(flat(hT_lo), mid[:, :], flat(hT_hi).bitcast(f32), ALU.subtract)\
                        .then_inc(s_hlo, 1)
                    after(1, (s_held, t + 1), (s_out, 16 * t))
                    nc.gpsimd.tensor_copy(id_rows[:, :], id_held[:, :]).then_inc(s_ids, 1)
                    after(2, (s_ids, t + 1))
                    nc.gpsimd.indirect_dma_start(
                        out=x2s[:, :], out_offset=None, in_=x2_dram[:, :, :].rearrange("g p n -> (g p) n"),
                        in_offset=bass.IndirectOffsetOnAxis(ap=id_rows[:, 0:1], axis=0),
                        bounds_check=G * P - 1, oob_is_err=False).then_inc(s_x2s, 16)

                nc.gpsimd.memset(x2s[:, :], 0.0).then_inc(s_clean, 1)
                eng.wait_ge(s_clean, 1)
                low_x(0)
                last_tile = tiles(eng, tile)
                out_rows(last_tile)
                eng.wait_ge(s_out, 16 * (last_tile + 1))

            @block.tensor
            def _(pe):
                def expert_of(t):
                    return pe.value_load(tile_q[0:1, blk(t)], min_val=0, max_val=E - 1)

                def x_in_array(t):
                    pe.wait_ge(s_xs, 16 * (t + 1))
                    wait(pe, s_xT, t)
                    for b in range(LB):
                        last = nc.tensor.transpose(x_bank[:, b * P:(b + 1) * P], xs[:, b * P:(b + 1) * P],
                                                   ident[:, :])
                    last.then_inc(s_xtr, 1)

                def project(bank, weights, slot, done):
                    for half in range(I // 512):
                        for b in range(LB):
                            hi = slot * (2 * MW) + (b * I + half * 512)
                            lo = slot * (2 * MW) + (MW + b * I + half * 512)
                            for n, (a, o) in enumerate(((xT_hi, hi), (xT_hi, lo), (xT_lo, hi))):
                                last = nc.tensor.matmul(bank[:, half * 512:(half + 1) * 512], a[:, b, :],
                                                        weights[:, bass.ds(o, 512)],
                                                        start=(b == 0 and n == 0), stop=(b == LB - 1 and n == 2))
                    last.then_inc(done, 1)

                def down(t):
                    q = expert_of(t)
                    pe.wait_ge(s_hlo, t + 1)
                    wait(pe, s_ys, t)
                    for b in range(IB):
                        if b % 2 == 0:
                            pe.wait_ge(s_ready[DOWN], q * CH + (b // 2 + 1))
                        for n, (a, w) in enumerate(((hT_hi, down_hi), (hT_hi, down_lo), (hT_lo, down_hi))):
                            last = nc.tensor.matmul(out_bank[:, :], a[:, b, :], w[:, b * 512:(b + 1) * 512],
                                                    start=(b == 0 and n == 0), stop=(b == IB - 1 and n == 2))
                    last.then_inc(s_down, 1)

                def tile(t):
                    q = expert_of(t)
                    slot = q % 2
                    pe.wait_ge(s_xlo, t + 1)
                    wait(pe, s_silu, t)
                    pe.wait_ge(s_ready[GATE], (q + 1) * CH)
                    project(gate_bank, gate, slot, s_gate)
                    wait(pe, s_upc, t)
                    pe.wait_ge(s_ready[UP], (q + 1) * CH)
                    project(up_bank, up, slot, s_up)
                    x_in_array(t + 1)
                    if known(t, lambda t: t > 0):
                        down(t - 1)
                    pe.wait_ge(s_hid, t + 1)
                    wait(pe, s_hT, t)
                    for b in range(IB):
                        last = nc.tensor.transpose(h_bank[b // LB][:, (b % LB) * P:(b % LB + 1) * P],
                                                   hid[:, b * P:(b + 1) * P], ident[:, :])
                    last.then_inc(s_htr, 1)

                x_in_array(0)
                last_tile = tiles(pe, tile)
                down(last_tile)


_NAMES = {
    "x_rows": "x", "ctx_cols": "ctx_2048", "skip": "fside_S2_0", "g_xattn": "g_xattn", "g_ffn": "g_ffn",
    "k": "L0_xattn_k", "router_w": "L0_ffn_router_w", "gate_w": "L0_ffn_gate_w", "up_w": "L0_ffn_up_w",
    "down_w": "L0_ffn_down_w",
}


def kernel(**inputs):
    import numpy as np
    import concourse.bacc as bacc
    from concourse import mybir as mb
    from concourse.bass_utils import run_bass_kernel_spmd

    nb, d, length = inputs["x"].shape
    groups = d // 16

    def by_group(a):
        a = np.asarray(a).reshape(nb, groups, 16, length).transpose(1, 0, 2, 3)
        return a.reshape(groups, nb * 16, length)

    arrays = {n: np.asarray(inputs[m]) for n, m in _NAMES.items()}
    arrays["x_rows"] = by_group(inputs["x"])
    cols = by_group(inputs["ctx_2048"]).reshape(groups, nb * 16, length // 128, 128)
    arrays["ctx_cols"] = cols.transpose(0, 3, 2, 1).reshape(groups, 128, length // 128 * nb * 16)
    nc = bacc.Bacc("TRN2", target_bir_lowering=False, num_devices=1)
    args = []
    for name, a in arrays.items():
        arrays[name] = a = np.ascontiguousarray(a)
        args.append(nc.dram_tensor(name, a.shape, mb.dt.from_np(a.dtype), kind="ExternalInput").ap())
    args.append(nc.dram_tensor("out", arrays["x_rows"].shape, mb.dt.float32, kind="ExternalOutput").ap())
    flamingo_layer_kernel(nc, *args)
    got = run_bass_kernel_spmd(nc, [arrays], core_ids=[0]).results[0]["out"]
    return got.reshape(groups, nb, 16, length).transpose(1, 0, 2, 3).reshape(nb, d, length)
```

```python
import concourse.bass as bass
from concourse import mybir
from contextlib import ExitStack


def flamingo_layer_kernel(
    nc: bass.Bass,
    x_rows: bass.AP,
    ctx_cols: bass.AP,
    skip: bass.AP,
    g_xattn: bass.AP,
    g_ffn: bass.AP,
    k: bass.AP,
    router_w: bass.AP,
    gate_w: bass.AP,
    up_w: bass.AP,
    down_w: bass.AP,
    out: bass.AP,
):
    f32 = mybir.dt.float32
    f32r = mybir.dt.float32r
    i32 = mybir.dt.int32
    ALU = mybir.AluOpType
    ACT = mybir.ActivationFunctionType
    AX = mybir.AxisListType.X

    P = 128
    G, _, L = x_rows.shape
    H = k.shape[0]
    J = 8
    NB = P // (2 * J)
    LB = L // P
    COL = NB * J * J
    E, _, I = gate_w.shape
    IB = I // P
    TILES = G + E - 1
    EPS = 1e-5
    assert 2 * (G - 2) >= TILES + 2
    NOBODY = 2 * G * P
    KPAD = P + L
    CH = 4
    CW = LB * I // CH
    MW = CH * CW

    kpad = nc.dram_tensor("kpad", [H, KPAD], f32)
    strips = nc.dram_tensor("strips", [H, P, L], f32)
    x2_dram = nc.dram_tensor("x2_dram", [G, P, L], f32)
    sorted_x = nc.dram_tensor("sorted_x", [2 * (G - 2) * P, L + 1], f32)

    base = (nc.sbuf_base + 31) // 32 * 32
    place = [base]

    def put(name, shape, dt=f32, at=None):
        size = 4
        for n in shape[1:]:
            size *= n
        size = (size + 31) // 32 * 32
        if at is None:
            at = place
        t = nc.alloc_sbuf_tensor_at(name, shape, dt, offset=at[0])
        at[0] += size
        return t

    ident = put("ident", [P, P])
    ones = put("ones", [P, P])
    upper = put("upper", [P, P])
    e_minus = put("e_minus", [P, E])
    iota_e = put("iota_e", [P, E])
    bounds = put("bounds", [P, G])
    iota_t = put("iota_t", [P, TILES])
    tanh_x = put("tanh_x", [P, 1])
    tanh_f = put("tanh_f", [P, 1])
    logits = put("logits", [P, G, E])
    pos = put("pos", [P, G], i32)
    tile_q = put("tile_q", [1, TILES], i32)
    load_e = put("load_e", [1, E], i32)
    end_q = put("end_q", [1, E], i32)
    mark_pool = put("mark_pool", [P, 3])
    mark_dve = put("mark_dve", [P, 1])
    mark_act = put("mark_act", [P, 1])
    n_used = put("n_used", [1, 2], i32)
    stats = put("stats", [P, 6])
    mv1 = put("mv1", [P, 2])
    ve1 = put("ve1", [P, 1])
    sd1 = put("sd1", [P, 1])
    rs1 = put("rs1", [P, 1])
    nb1 = put("nb1", [P, 1])
    mv2 = put("mv2", [P, 2])
    ve2 = put("ve2", [P, 1])
    sd2 = put("sd2", [P, 1])
    rs2 = put("rs2", [P, 1])
    nb2 = put("nb2", [P, 1])
    raw_at = place[0]
    raw = put("raw", [P, CH, CW])
    gate_at = place[0]
    gate = put("gate", [P, 4 * MW], f32r)
    place[0] += 4 * G
    up_at = place[0]
    up = put("up", [P, 4 * MW], f32r)
    down_at = place[0]
    down_hi = put("down_hi", [P, MW], f32r)
    down_lo = put("down_lo", [P, MW], f32r)
    xs = put("xs", [P, L + 1])
    xT_raw = put("xT_raw", [P, LB * P])
    xT_hi = put("xT_hi", [P, LB, P], f32r)
    xT_lo = put("xT_lo", [P, LB, P], f32r)
    hid = put("hid", [P, I])
    mid = put("mid", [P, I])
    hT_hi = put("hT_hi", [P, IB, P], f32r)
    hT_lo = put("hT_lo", [P, IB, P], f32r)
    ys = put("ys", [P, L])
    x2s = put("x2s", [P, L])
    id_next = put("id_next", [P, 2])
    id_held = put("id_held", [P, 1])
    id_rows = put("id_rows", [P, 1], i32)

    xn_all = put("xn_all", [P, G, L + 1], f32, [gate_at + 2 * MW * 4])

    low = [raw_at]
    kv = put("kv", [P, 2, LB * COL], f32, low)
    kv_hi = put("kv_hi", [P, 2, 2, LB * COL], f32r, low)
    assert low[0] <= gate_at + 2 * MW * 4
    att = [up_at]
    kv_lo = put("kv_lo", [P, 2, 2, LB * COL], f32r, att)
    prod = put("prod", [P, 2, J + 1, LB * P], f32, att)
    t_raw = put("t_raw", [P, 2, L], f32, att)
    t_hi = put("t_hi", [P, 2, 2, L], f32r, att)
    t_lo = put("t_lo", [P, 2, 2, L], f32r, att)
    x_in = put("x_in", [P, 2, L], f32, att)
    x_res = put("x_res", [P, 2, L], f32, att)
    xn = put("xn", [P, L], f32, att)
    xn2 = put("xn2", [P, L], f32, att)
    xn2T = put("xn2T", [P, LB, P], f32, att)
    vT = put("vT", [P, 2, LB * P], f32, att)
    cT = put("cT", [P, 2, LB * P], f32, att)
    cK = put("cK", [P, 2, LB * P], f32, att)
    vc = put("vc", [P, LB * P], f32, att)
    skip_b = put("skip_b", [P, G * 2 * J], f32, att)
    skip_w = put("skip_w", [P, LB * NB, 2], f32, att)
    router = put("router", [P, LB, E], f32, att)
    fill = put("fill", [P, L + 1], f32, att)

    rt = [up_at + 2 * MW * 4]
    best = put("best", [P, G], f32, rt)
    hot = put("hot", [P, G, E], f32, rt)
    cand = put("cand", [P, G, E], f32, rt)
    pick = put("pick", [P, G], f32, rt)
    scan_a = put("scan_a", [P, G, E], f32, rt)
    scan_b = put("scan_b", [P, G, E], f32, rt)
    total = put("total", [P, G, E], f32, rt)
    over = put("over", [P, E, G], f32, rt)
    n_tiles = put("n_tiles", [P, E], f32, rt)
    ends = [put(f"ends{n}", [P, E], f32, rt) for n in range(3)]
    used = put("used", [P, E], f32, rt)
    ranks = [put(f"ranks{n}", [P, E], f32, rt) for n in range(3)]
    base_e = put("base_e", [P, E], f32, rt)
    pos_f = put("pos_f", [P, G], f32, rt)
    match = put("match", [P, E, E], f32, rt)
    match2 = put("match2", [P, E, E], f32, rt)
    sel_e = put("sel_e", [P, E], f32, rt)
    sel_end = put("sel_end", [P, E], f32, rt)
    last_q = put("last_q", [P, E], f32, rt)
    past = put("past", [P, TILES, E], f32, rt)
    tq_f = put("tq_f", [P, TILES], f32, rt)
    place_1 = put("place_1", [P, G], f32, rt)
    places = put("places", [P, P], f32, rt)
    select = put("select", [P, G, P], f32, rt)

    ctx = ExitStack()
    with ctx:
        def sem(name):
            return ctx.enter_context(nc.semaphore(name))

        psum = [ctx.enter_context(nc.psum_tensor(f"bank{n}", [P, 512], f32)) for n in range(4)]
        pairs = [ctx.enter_context(nc.psum_tensor(f"pair{n}", [P, 1024], f32)) for n in range(2)]

        y_bank = psum
        v_bank = pairs[0][:, 0:512]
        att_bank = pairs[0][:, 512:1024]
        x2T_bank = pairs[1][:, 0:512]
        log_bank = pairs[1][:, 512:512 + E]

        s_const = sem("s_const")
        s_kzero = sem("s_kzero")
        s_kcopy = sem("s_kcopy")
        s_strip = [sem(f"s_strip{n}") for n in range(4)]
        s_zfill = sem("s_zfill")
        s_small = sem("s_small")
        s_gates = sem("s_gates")
        s_tanh = sem("s_tanh")
        s_x = [sem(f"s_x{n}") for n in range(2)]
        s_c = [sem(f"s_c{n}") for n in range(2)]
        s_cK = [sem(f"s_cK{n}") for n in range(2)]
        s_r = [sem(f"s_r{n}") for n in range(2)]
        s_t = sem("s_t")
        s_x2st = [sem(f"s_x2st{n}") for n in range(2)]
        s_xnc = sem("s_xnc")
        s_wraw = [sem(f"s_wraw{n}") for n in range(CH)]
        s_whi = sem("s_whi")
        s_var1 = sem("s_var1")
        s_sd1 = sem("s_sd1")
        s_nb1 = sem("s_nb1")
        s_xn = sem("s_xn")
        s_vtr = sem("s_vtr")
        s_vT = sem("s_vT")
        s_thi = sem("s_thi")
        s_tlo = sem("s_tlo")
        s_kv = sem("s_kv")
        s_khi = sem("s_khi")
        s_klo = sem("s_klo")
        s_skip = sem("s_skip")
        s_skv = sem("s_skv")
        s_skw = sem("s_skw")
        s_skp = sem("s_skp")
        s_y = sem("s_y")
        s_p = sem("s_p")
        s_add = sem("s_add")
        s_add2 = sem("s_add2")
        s_att = sem("s_att")
        s_x2 = sem("s_x2")
        s_var2 = sem("s_var2")
        s_sd2 = sem("s_sd2")
        s_nb2 = sem("s_nb2")
        s_xn2 = sem("s_xn2")
        s_x2tr = sem("s_x2tr")
        s_xn2T = sem("s_xn2T")
        s_log = sem("s_log")
        s_logc = sem("s_logc")
        s_ln1 = sem("s_ln1")
        s_ln2 = sem("s_ln2")

        def wait(eng, s, value):
            if isinstance(value, int) and value <= 0:
                return
            eng.wait_ge(s, value)

        def stages(eng, body):
            body(0, 0, 0)
            body(1, 1, 0)
            with eng.Fori(1, G // 2 - 1) as pair:
                body(2 * pair, 0, pair)
                body(2 * pair + 1, 1, pair)
            body(G - 2, 0, G // 2 - 1)
            body(G - 1, 1, G // 2 - 1)

        def blk(g, size=1):
            if isinstance(g, int):
                return slice(g * size, (g + 1) * size)
            return bass.ds(g * size, size)

        def known(g, test):
            return test(g) if isinstance(g, int) else True

        s_ready = [sem(f"s_ready_{n}") for n in ("gate", "up", "down")]

        def weight_chunk(kind, e, c):
            if kind < 2:
                w = gate_w if kind == 0 else up_w
                return w[blk(e), c * P:(c + 1) * P, :].rearrange("o p n -> (o p) n")
            rows = down_w[blk(e), 2 * c * P:(2 * c + 2) * P, :]
            return rows.rearrange("o (k p) n -> p (o k) n", p=P)

        def raw_chunk(kind, c):
            return raw[:, c, :] if kind < 2 else raw[:, c, :].rearrange("p (k n) -> p k n", k=2)

        GATE, UP, DOWN = range(3)

        def load_matrix(eng, kind, e, before=None, q_before=0):
            for c in range(CH):
                if before is not None:
                    eng.wait_ge(s_ready[before], q_before * CH + (c + 1))
                eng.dma_start(raw_chunk(kind, c), weight_chunk(kind, e, c)).then_inc(s_wraw[c], 16)


        def slot_parts(kind, slot, c):
            if kind == 2:
                return down_hi[:, c * CW:(c + 1) * CW], down_lo[:, c * CW:(c + 1) * CW]
            w = gate if kind == 0 else up
            o = slot * 2 * MW + c * CW
            return w[:, o:o + CW], w[:, o + MW:o + MW + CW]

        def outer_product(engine, u, hh):
            v = vT[:, u, :].rearrange("p (a r) -> p a r", r=2 * J)[:, :, hh * J:(hh + 1) * J]
            c = cK[:, u, :].rearrange("p (a r) -> p a r", r=2 * J)[:, :, hh * J:(hh + 1) * J]
            engine.tensor_tensor(
                kv[:, hh, :].rearrange("p (a i j) -> p a i j", i=J, j=J),
                v.unsqueeze(3).broadcast_to([P, LB * NB, J, J]),
                c.unsqueeze(2).broadcast_to([P, LB * NB, J, J]), ALU.mult).then_inc(s_kv, 1)

        with nc.Block() as block:

            @block.sync
            def _(eng):
                def rows(dram, g):
                    return dram[blk(g), :, :].rearrange("o p n -> (o p) n")

                def load_x(g, u, n):
                    wait(eng, s_xn, g - 1)
                    eng.dma_start(x_in[:, u, :], rows(x_rows, g)).then_inc(s_x[u], 16)

                def load_cK(g, u):
                    wait(eng, s_kv, 2 * (g - 1))
                    wait(eng, s_skip, g - 1)
                    eng.dma_start(cK[:, u, :], rows(ctx_cols, g)).then_inc(s_cK[u], 16)

                def load_cT(g, u):
                    wait(eng, s_p, (g - 1) * 2 * LB)
                    wait(eng, s_skp, g - 1)
                    eng.dma_start(cT[:, u, :], rows(ctx_cols, g)).then_inc(s_c[u], 16)

                def strip_of(g):
                    return bass.AP(kpad, 2 * g * KPAD + P, [[KPAD, 2], [-1, P], [1, L]])

                STRIP_PARTS = [range(1), range(1, 2), range(2, G // 2), range(G // 2, G)]

                def make_strips(part):
                    for a in STRIP_PARTS[part]:
                        eng.dma_start(strips[2 * a:2 * a + 2, :, :], strip_of(a)).then_inc(s_strip[part], 16)

                def load_t(g):
                    wait(eng, s_thi, g)
                    wait(eng, s_tlo, g)
                    part = 3 if not isinstance(g, int) or g >= G // 2 else min(g, 2)
                    eng.wait_ge(s_strip[part], 16 * len(STRIP_PARTS[part]))
                    eng.dma_start(t_raw[:, :, :], strips[blk(g, 2), :, :].rearrange("h p n -> p h n"))\
                       .then_inc(s_t, 16)

                def store_x2(g, u):
                    eng.wait_ge(s_x2, g + 1)
                    eng.dma_start(rows(x2_dram, g), x_res[:, u, :]).then_inc(s_x2st[u], 16)

                def stage(g, u, n):
                    if known(g, lambda g: g < G - 2):
                        load_x(g + 2, u, n)
                    if known(g, lambda g: g < G - 1):
                        load_cK(g + 1, 1 - u)
                    load_cT(g, u)
                    if known(g, lambda g: g < G - 1):
                        load_t(g + 1)
                    if known(g, lambda g: g >= 2):
                        store_x2(g - 2, u)
                        eng.wait_ge(s_x2st[u], 16 * n)
                        eng.wait_ge(s_xn2, g - 1)
                    eng.dma_start(x_res[:, u, :], rows(x_rows, g)).then_inc(s_r[u], 16)
                    if isinstance(g, int) and g < 2:
                        make_strips(2 + g)
                    if known(g, lambda g: g >= 2):
                        eng.dma_start(sorted_x[blk(g - 2, 2 * P), :].rearrange("(k p) n -> p k n", p=P),
                                      fill[:, :].unsqueeze(1).broadcast_to([P, 2, L + 1])).then_inc(s_zfill, 16)

                eng.dma_start(kpad[:, P:KPAD], k).then_inc(s_kcopy, 16)
                load_x(0, 0, 0)
                eng.wait_ge(s_const, 1)
                eng.dma_start(kpad[:, 0:P], fill[0:H, 0:P]).then_inc(s_kzero, 16)
                load_x(1, 1, 0)
                load_cK(0, 0)
                eng.wait_ge(s_kcopy, 16)
                eng.wait_ge(s_kzero, 16)
                make_strips(0)
                load_t(0)
                eng.dma_start(skip_b[:, :], bass.AP(skip.tensor, 0, [[0, P], [1, G * 2 * J]])).then_inc(s_small, 16)
                eng.dma_start(router[:, :, :], router_w.rearrange("(b p) e -> p b e", p=P)).then_inc(s_small, 16)
                make_strips(1)
                eng.wait_ge(s_const, 2)
                stages(eng, stage)
                for g in (G - 2, G - 1):
                    store_x2(g, g % 2)
                for u in range(2):
                    eng.wait_ge(s_x2st[u], 16 * (G // 2))
                eng.wait_ge(s_zfill, 16 * (G - 2))

            @block.gpsimd
            def _(eng):
                nc.gpsimd.memset(fill[:, 0:L], 0.0).then_inc(s_const, 1)
                nc.gpsimd.memset(fill[:, L:L + 1], float(NOBODY)).then_inc(s_const, 1)
                nc.gpsimd.memset(ident[:, :], 0.0).then_inc(s_const, 1)
                nc.gpsimd.memset(ones[:, :], 1.0).then_inc(s_const, 1)
                eng.wait_ge(s_const, 4)
                nc.gpsimd.affine_select(out=ident[:, :], in_=ident[:, :], compare_op=ALU.not_equal, fill=1.0,
                                        base=0, pattern=[[-1, P]], channel_multiplier=1).then_inc(s_const, 1)
                nc.gpsimd.affine_select(out=upper[:, :], in_=ones[:, :], compare_op=ALU.is_gt, fill=0.0,
                                        base=0, pattern=[[1, P]], channel_multiplier=-1).then_inc(s_const, 1)
                for t, base0, step in ((e_minus, 1 - E, 1), (iota_e, 0, 1), (bounds, 0, P), (iota_t, 0, 1)):
                    nc.gpsimd.iota(t[:, :], pattern=[[step, t.shape[1]]], base=base0, channel_multiplier=0,
                                   allow_small_or_imprecise_dtypes=True).then_inc(s_const, 1)
                nc.gpsimd.iota(xn_all[:, :, L:L + 1], pattern=[[P, G]], base=0, channel_multiplier=1,
                               allow_small_or_imprecise_dtypes=True).then_inc(s_const, 1)

                def outer(g, u, n, hh):
                    h = 2 * g + hh
                    if hh == 0:
                        eng.wait_ge(s_vT, g + 1)
                        eng.wait_ge(s_cK[u], 16 * (n + 1))
                    wait(eng, s_khi, h - 1)
                    wait(eng, s_klo, h - 1)
                    outer_product(nc.gpsimd, u, hh)

                def skip_first(g, u):
                    a = LB * NB
                    wait(eng, s_skw, g)
                    wait(eng, s_skip, g)
                    s_g = skip_b[:, blk(g, 2 * J)]
                    nc.gpsimd.tensor_tensor(
                        vc[:, :].rearrange("p (a r) -> p a r", r=2 * J),
                        vT[:, u, :].rearrange("p (a r) -> p a r", r=2 * J),
                        s_g.unsqueeze(1).broadcast_to([P, a, 2 * J]), ALU.mult).then_inc(s_skv, 1)
                    eng.wait_ge(s_skv, g + 1)
                    nc.gpsimd.tensor_tensor(vc[:, :], vc[:, :], cK[:, u, :], ALU.mult).then_inc(s_skip, 1)

                def skip_last(g, u, n):
                    eng.wait_ge(s_skw, g + 1)
                    eng.wait_ge(s_c[u], 16 * (n + 1))
                    wait(eng, s_att, g - 1)
                    nc.gpsimd.tensor_tensor(
                        prod[:, u, J, :].rearrange("p (a h j) -> p a h j", h=2, j=J),
                        cT[:, u, :].rearrange("p (a h j) -> p a h j", h=2, j=J),
                        skip_w[:, :, :].unsqueeze(3).broadcast_to([P, LB * NB, 2, J]), ALU.mult)\
                        .then_inc(s_skp, 1)

                def add_pairs(g, u, hh):
                    eng.wait_ge(s_p, (2 * g + hh + 1) * LB)
                    terms = prod[:, u, 0:J, :].rearrange("p i (a r) -> p i a r", r=2 * J)[:, :, :, hh * J:(hh + 1) * J]
                    nc.gpsimd.tensor_tensor(terms[:, 0:J // 2], terms[:, 0:J // 2], terms[:, J // 2:J], ALU.add)\
                        .then_inc(s_add, 1)

                def before_conv(g, u, n):
                    if isinstance(g, int) and g == 0:
                        eng.wait_ge(s_small, 32)
                        eng.wait_ge(s_kv, 1)
                    else:
                        outer(g, u, n, 0)
                    skip_first(g, u)
                    outer(g, u, n, 1)

                def stage(g, u, n):
                    if known(g, lambda g: g >= 1):
                        add_pairs(g - 1, 1 - u, 1)
                    skip_last(g, u, n)
                    if known(g, lambda g: g < G - 1):
                        before_conv(g + 1, 1 - u, n + u)
                    add_pairs(g, u, 0)

                before_conv(0, 0, 0)
                stages(eng, stage)

            @block.scalar
            def _(act):
                def root1(g):
                    act.wait_ge(s_var1, g + 1)
                    nc.scalar.activation(sd1[:, :], ve1[:, :], ACT.Sqrt).then_inc(s_sd1, 1)

                def norm(dst, src, rs, nb, done):
                    nc.scalar.activation(dst, src, ACT.Identity, bias=nb[:, 0:1], scale=rs[:, 0:1]).then_inc(done, 1)

                def norm1(g, u):
                    act.wait_ge(s_nb1, g + 1)
                    wait(act, s_vtr, g)
                    norm(xn[:, :], x_in[:, u, :], rs1, nb1, s_xn)

                def norm2(g, u):
                    act.wait_ge(s_nb2, g + 1)
                    wait(act, s_x2tr, g)
                    wait(act, s_xnc, g)
                    norm(xn2[:, :], x_res[:, u, :], rs2, nb2, s_xn2)

                def strip_hi(g, u):
                    act.wait_ge(s_t, 16 * (g + 1))
                    wait(act, s_y, (g - 1) * 2 * LB)
                    nc.scalar.activation(t_hi[:, u, :, :], t_raw[:, :, :], ACT.Copy).then_inc(s_thi, 1)

                def v_out(g, u):
                    act.wait_ge(s_vtr, g + 1)
                    wait(act, s_kv, 2 * (g - 1))
                    wait(act, s_skip, g - 1)
                    nc.scalar.activation(vT[:, u, :], v_bank, ACT.Copy).then_inc(s_vT, 1)

                def kv_high(g, u, hh):
                    h = 2 * g + hh
                    act.wait_ge(s_kv, h + 1)
                    wait(act, s_y, (h - 3) * LB)
                    nc.scalar.activation(kv_hi[:, u, hh, :], kv[:, hh, :], ACT.Copy).then_inc(s_khi, 1)

                def logits_out(g):
                    act.wait_ge(s_log, g + 1)
                    nc.scalar.activation(logits[:, blk(g), :].rearrange("p o e -> p (o e)"), log_bank, ACT.Copy)\
                        .then_inc(s_logc, 1)

                def root2(g):
                    act.wait_ge(s_var2, g + 1)
                    nc.scalar.activation(sd2[:, :], ve2[:, :], ACT.Sqrt).then_inc(s_sd2, 1)

                def xn2T_out(g):
                    act.wait_ge(s_x2tr, g + 1)
                    wait(act, s_log, g)
                    nc.scalar.activation(xn2T[:, :, :].rearrange("p b t -> p (b t)"), x2T_bank, ACT.Copy)\
                        .then_inc(s_xn2T, 1)

                def xn2_out(g):
                    act.wait_ge(s_xn2, g + 1)
                    nc.scalar.activation(xn_all[:, blk(g), 0:L].rearrange("p o n -> p (o n)"), xn2[:, :], ACT.Copy)\
                        .then_inc(s_xnc, 1)

                def stage(g, u, n):
                    more = known(g, lambda g: g < G - 1)
                    before = known(g, lambda g: g >= 1)
                    if known(g, lambda g: g < G - 2):
                        root1(g + 2)
                        norm1(g + 2, u)
                    if more:
                        kv_high(g + 1, 1 - u, 0)
                    if known(g, lambda g: g >= 2):
                        logits_out(g - 2)
                    if more:
                        strip_hi(g + 1, 1 - u)
                    if before:
                        root2(g - 1)
                        norm2(g - 1, 1 - u)
                    if more:
                        kv_high(g + 1, 1 - u, 1)
                    if known(g, lambda g: g < G - 2):
                        v_out(g + 2, u)
                    if before:
                        xn2_out(g - 1)
                        xn2T_out(g - 1)

                act.dma_start(tanh_x[:, :], bass.AP(g_xattn.tensor, 0, [[0, P], [1, 1]])).then_inc(s_gates, 16)
                act.dma_start(tanh_f[:, :], bass.AP(g_ffn.tensor, 0, [[0, P], [1, 1]])).then_inc(s_gates, 16)
                act.wait_ge(s_gates, 32)
                nc.scalar.activation(tanh_x[:, :], tanh_x[:, :], ACT.Tanh).then_inc(s_tanh, 1)
                nc.scalar.activation(tanh_f[:, :], tanh_f[:, :], ACT.Tanh).then_inc(s_tanh, 1)
                root1(0)
                norm1(0, 0)
                v_out(0, 0)
                root1(1)
                norm1(1, 1)
                strip_hi(0, 0)
                kv_high(0, 0, 0)
                v_out(1, 1)
                kv_high(0, 0, 1)
                stages(act, stage)
                logits_out(G - 2)
                root2(G - 1)
                norm2(G - 1, 1)
                xn2T_out(G - 1)
                logits_out(G - 1)
                xn2_out(G - 1)

            @block.vector
            def _(dve):
                def norm_first(src, mv, ve, done, steps, g):
                    nc.vector.bn_stats(stats[:, :], src).then_inc(steps, 1)
                    dve.wait_ge(steps, 3 * g + 1)
                    nc.vector.tensor_copy(mark_dve[:, :], stats[:, 0:1])
                    nc.vector.bn_aggr(mv[:, :], stats[:, :]).then_inc(steps, 1)
                    dve.wait_ge(steps, 3 * g + 2)
                    nc.vector.tensor_scalar(ve[:, :], mv[:, 1:2], EPS, None, ALU.add).then_inc(done, 1)

                def norm_last(mv, sd, rs, nb, s_sd, s_norm, done, steps, g):
                    dve.wait_ge(s_sd, g + 1)
                    wait(dve, s_norm, g)
                    nc.vector.reciprocal(rs[:, :], sd[:, :]).then_inc(steps, 1)
                    dve.wait_ge(steps, 3 * g + 3)
                    nc.vector.tensor_scalar(nb[:, :], mv[:, 0:1], rs[:, 0:1], -1.0, ALU.mult, ALU.mult)\
                        .then_inc(done, 1)

                def ln1(g, u, n):
                    dve.wait_ge(s_x[u], 16 * (n + 1))
                    norm_first(x_in[:, u, :], mv1, ve1, s_var1, s_ln1, g)
                    norm_last(mv1, sd1, rs1, nb1, s_sd1, s_xn, s_nb1, s_ln1, g)

                def strip_lo(g, u):
                    dve.wait_ge(s_thi, g + 1)
                    wait(dve, s_y, (g - 1) * 2 * LB)
                    nc.vector.tensor_tensor(t_lo[:, u, :, :], t_raw[:, :, :], t_hi[:, u, :, :].bitcast(f32),
                                            ALU.subtract).then_inc(s_tlo, 1)

                def kv_low(g, u, hh):
                    h = 2 * g + hh
                    dve.wait_ge(s_khi, h + 1)
                    wait(dve, s_y, (h - 3) * LB)
                    nc.vector.tensor_tensor(kv_lo[:, u, hh, :], kv[:, hh, :], kv_hi[:, u, hh, :].bitcast(f32),
                                            ALU.subtract).then_inc(s_klo, 1)

                def product(g, u, n, hh, lb):
                    h = 2 * g + hh
                    if hh == 0 and lb == 0:
                        dve.wait_ge(s_c[u], 16 * (n + 1))
                        wait(dve, s_att, g - 1)
                    dve.wait_ge(s_y, h * LB + lb + 1)
                    c = cT[:, u, lb * P:(lb + 1) * P].rearrange("p (b r) -> p b r", r=2 * J)
                    c = c[:, :, hh * J:(hh + 1) * J].unsqueeze(3).broadcast_to([P, NB, J, J])
                    dst = prod[:, u, 0:J, lb * P:(lb + 1) * P].rearrange("p i (b r) -> p b i r", r=2 * J)
                    nc.vector.tensor_tensor(dst[:, :, :, hh * J:(hh + 1) * J],
                                            y_bank[lb][:, :].rearrange("p (b i j) -> p b i j", i=J, j=J),
                                            c, ALU.mult).then_inc(s_p, 1)

                def residual(g, u, n):
                    dve.wait_ge(s_att, g + 1)
                    dve.wait_ge(s_r[u], 16 * (n + 1))
                    nc.vector.scalar_tensor_tensor(out=x_res[:, u, :], in0=att_bank, scalar=tanh_x[:, 0:1],
                                                   in1=x_res[:, u, :], op0=ALU.mult, op1=ALU.add)\
                        .then_inc(s_x2, 1)

                def ln2_first(g, u):
                    dve.wait_ge(s_x2, g + 1)
                    norm_first(x_res[:, u, :], mv2, ve2, s_var2, s_ln2, g)

                def ln2_last(g):
                    norm_last(mv2, sd2, rs2, nb2, s_sd2, s_xn2, s_nb2, s_ln2, g)

                def add_last_pairs(g, u):
                    dve.wait_ge(s_add, 2 * g + 1)
                    dve.wait_ge(s_p, (g + 1) * 2 * LB)
                    terms = prod[:, u, 0:J, :].rearrange("p i (a r) -> p i a r", r=2 * J)[:, :, :, J:2 * J]
                    nc.vector.tensor_tensor(terms[:, 0:J // 2], terms[:, 0:J // 2], terms[:, J // 2:J], ALU.add)\
                        .then_inc(s_add, 1)

                def add_fours(g, u):
                    dve.wait_ge(s_add, 2 * (g + 1))
                    nc.vector.tensor_tensor(prod[:, u, 0:2, :], prod[:, u, 0:2, :], prod[:, u, 2:4, :], ALU.add)\
                        .then_inc(s_add2, 1)

                def skip_sum(g):
                    dve.wait_ge(s_skip, g + 1)
                    wait(dve, s_skp, g)
                    nc.vector.tensor_reduce(skip_w[:, :, :],
                                            vc[:, :].rearrange("p (a h i) -> p a h i", h=2, i=J), AX, ALU.add)\
                        .then_inc(s_skw, 1)

                def stage(g, u, n):
                    more = known(g, lambda g: g < G - 1)
                    before = known(g, lambda g: g >= 1)
                    product(g, u, n, 0, 0)
                    product(g, u, n, 0, 1)
                    if before:
                        add_fours(g - 1, 1 - u)
                    if known(g, lambda g: g < G - 2):
                        ln1(g + 2, u, n + 1)
                    product(g, u, n, 0, 2)
                    product(g, u, n, 0, 3)
                    if before:
                        residual(g - 1, 1 - u, n - 1 + u)
                        ln2_first(g - 1, 1 - u)
                    if more:
                        kv_low(g + 1, 1 - u, 0)
                    if before:
                        ln2_last(g - 1)
                    if more:
                        strip_lo(g + 1, 1 - u)
                    product(g, u, n, 1, 0)
                    product(g, u, n, 1, 1)
                    if more:
                        skip_sum(g + 1)
                    product(g, u, n, 1, 2)
                    product(g, u, n, 1, 3)
                    if more:
                        kv_low(g + 1, 1 - u, 1)

                ln1(0, 0, 0)
                ln1(1, 1, 0)
                dve.wait_ge(s_vT, 1)
                dve.wait_ge(s_cK[0], 16)
                outer_product(nc.vector, 0, 0)
                strip_lo(0, 0)
                kv_low(0, 0, 0)
                skip_sum(0)
                kv_low(0, 0, 1)
                dve.wait_ge(s_tanh, 2)
                stages(dve, stage)
                add_last_pairs(G - 1, 1)
                add_fours(G - 1, 1)
                residual(G - 1, 1, G // 2 - 1)
                ln2_first(G - 1, 1)
                ln2_last(G - 1)

            @block.tensor
            def _(pe):
                def transposes(bank, src, done):
                    for b in range(LB):
                        last = nc.tensor.transpose(bank[:, b * P:(b + 1) * P], src[:, b * P:(b + 1) * P],
                                                   ident[:, :])
                    last.then_inc(done, 1)

                def v_in(g):
                    pe.wait_ge(s_xn, g + 1)
                    wait(pe, s_vT, g)
                    transposes(v_bank, xn, s_vtr)

                def conv(g, u, hh, blocks):
                    h = 2 * g + hh
                    for lb in blocks:
                        if lb == 0:
                            pe.wait_ge(s_klo, h + 1)
                            if hh == 0:
                                pe.wait_ge(s_tlo, g + 1)
                        wait(pe, s_p, (h - 1) * LB + lb + 1)
                        for mb in range(lb + 1):
                            d = lb - mb
                            for n, (t, v) in enumerate(((t_hi, kv_hi), (t_hi, kv_lo), (t_lo, kv_hi))):
                                last = nc.tensor.matmul(
                                    y_bank[lb][:, :], t[:, u, hh, d * P:(d + 1) * P],
                                    v[:, u, hh, mb * COL:(mb + 1) * COL],
                                    start=(mb == 0 and n == 0), stop=(mb == lb and n == 2))
                        last.then_inc(s_y, 1)

                def logits_of(g):
                    pe.wait_ge(s_xn2T, g + 1)
                    wait(pe, s_logc, g)
                    for b in range(LB):
                        last = nc.tensor.matmul(log_bank, xn2T[:, b, :], router[:, b, :],
                                                start=(b == 0), stop=(b == LB - 1))
                    last.then_inc(s_log, 1)

                def sum_heads(g, u):
                    pe.wait_ge(s_add2, g + 1)
                    pe.wait_ge(s_skp, g + 1)
                    wait(pe, s_x2, g)
                    terms = [0, 1, J]
                    for lb in range(LB):
                        for i in terms:
                            last = nc.tensor.matmul(att_bank[:, lb * P:(lb + 1) * P],
                                                    prod[:, u, i, lb * P:(lb + 1) * P], ident[:, :],
                                                    start=(i == 0), stop=(i == J), is_transpose=True)
                    last.then_inc(s_att, 1)

                def x2_in(g):
                    pe.wait_ge(s_xn2, g + 1)
                    wait(pe, s_xn2T, g)
                    transposes(x2T_bank, xn2, s_x2tr)

                def stage(g, u, n):
                    before = known(g, lambda g: g >= 1)
                    conv(g, u, 0, (0, 1, 2))
                    if known(g, lambda g: g >= 2):
                        logits_of(g - 2)
                    conv(g, u, 0, (3,))
                    if before:
                        sum_heads(g - 1, 1 - u)
                    conv(g, u, 1, (0, 1, 2))
                    if known(g, lambda g: g < G - 2):
                        v_in(g + 2)
                    conv(g, u, 1, (3,))
                    if before:
                        x2_in(g - 1)

                pe.wait_ge(s_const, 6)
                v_in(0)
                v_in(1)
                stages(pe, stage)
                logits_of(G - 2)
                sum_heads(G - 1, 1)
                x2_in(G - 1)
                logits_of(G - 1)

        s_hot = sem("s_hot")
        s_cnt = sem("s_cnt")
        s_pos = sem("s_pos")
        s_tab = sem("s_tab")
        s_places = sem("s_places")
        s_sel = sem("s_sel")
        s_sorted = sem("s_sorted")
        s_scat = [sem(f"s_scat{n}") for n in range(G)]
        s_rt = sem("s_rt")

        def routing_loads(eng):
            load_matrix(eng, GATE, 0)
            load_matrix(eng, UP, 0, GATE, 0)
            eng.wait_ge(s_sorted, 1)
            load_matrix(eng, DOWN, 0, UP, 0)

        def first_high_parts(act, kind, chunks):
            for c in chunks:
                act.wait_ge(s_wraw[c], 16 * (kind + 1))
                nc.scalar.activation(slot_parts(kind, 0, c)[0], raw[:, c, :], ACT.Copy).then_inc(s_whi, 1)

        def first_low_parts(dve, kind, chunks):
            for c in chunks:
                hi, lo = slot_parts(kind, 0, c)
                dve.wait_ge(s_whi, kind * CH + c + 1)
                nc.vector.tensor_tensor(lo, raw[:, c, :], hi.bitcast(f32), ALU.subtract).then_inc(s_ready[kind], 1)

        def routing_counts(pe):
            pe.wait_ge(s_hot, 1)
            flat = hot[:, :, :].rearrange("p g e -> p (g e)")
            nc.tensor.matmul(psum[0][:, 0:G * E], upper[:, :], flat, start=True, stop=True)
            nc.tensor.matmul(psum[1][:, 0:G * E], ones[:, :], flat, start=True, stop=True).then_inc(s_cnt, 1)

        def routing(dve):
            done = [0]

            def step(instruction):
                done[0] += 1
                instruction.then_inc(s_rt, 1)
                dve.wait_ge(s_rt, done[0])

            V = nc.vector
            ge = [P, G, E]
            step(V.tensor_reduce(best[:, :], logits[:, :, :], AX, ALU.max))
            step(V.tensor_tensor(cand[:, :, :], logits[:, :, :], best[:, :].unsqueeze(2).broadcast_to(ge),
                                 ALU.is_equal))
            step(V.tensor_tensor(hot[:, :, :], cand[:, :, :], e_minus[:, :].unsqueeze(1).broadcast_to(ge),
                                 ALU.mult))
            step(V.tensor_reduce(pick[:, :], hot[:, :, :], AX, ALU.min))
            V.tensor_tensor(hot[:, :, :], e_minus[:, :].unsqueeze(1).broadcast_to(ge),
                            pick[:, :].unsqueeze(2).broadcast_to(ge), ALU.is_equal).then_inc(s_hot, 1)
            dve.wait_ge(s_cnt, 1)
            step(V.tensor_copy(total[:, :, :], psum[1][:, 0:G * E].rearrange("p (g e) -> p g e", e=E)))
            src, dst = total, scan_a
            shift = 1
            while shift < G:
                V.tensor_copy(dst[:, 0:shift, :], src[:, 0:shift, :])
                step(V.tensor_tensor(dst[:, shift:G, :], src[:, shift:G, :], src[:, 0:G - shift, :], ALU.add))
                src, dst = dst, (scan_b if dst is scan_a else scan_a)
                shift *= 2
            counts = src[:, G - 1, :]
            step(V.tensor_tensor(dst[:, :, :], src[:, :, :], total[:, :, :], ALU.subtract))
            step(V.tensor_tensor(dst[:, :, :], psum[0][:, 0:G * E].rearrange("p (g e) -> p g e", e=E),
                                 dst[:, :, :], ALU.add))
            step(V.scalar_tensor_tensor(out=place_1[:, :], in0=dst[:, :, 0], scalar=1.0, in1=hot[:, :, 0],
                                        op0=ALU.add, op1=ALU.mult))
            dve.wait_ge(s_places, 1)
            for g in range(G):
                V.tensor_scalar(select[:, g, :], places[:, :], place_1[:, g:g + 1], None, ALU.is_equal)\
                    .then_inc(s_sel, 1)
            step(V.tensor_tensor(over[:, :, :], counts.unsqueeze(2).broadcast_to([P, E, G]),
                                 bounds[:, :].unsqueeze(1).broadcast_to([P, E, G]), ALU.is_gt))
            step(V.tensor_reduce(n_tiles[:, :], over[:, :, :], AX, ALU.add))
            step(V.tensor_scalar(n_tiles[:, 0:1], n_tiles[:, 0:1], 1.0, None, ALU.max))

            def sums(steps):
                for n, shift in enumerate((1, 2, 4)):
                    V.tensor_copy(steps[n + 1][:, 0:shift], steps[n][:, 0:shift])
                    step(V.tensor_tensor(steps[n + 1][:, shift:E], steps[n][:, shift:E],
                                         steps[n][:, 0:E - shift], ALU.add))
                return steps[3]

            end_e = sums([n_tiles, *ends])
            step(V.tensor_tensor(base_e[:, :], end_e[:, :], n_tiles[:, :], ALU.subtract))
            step(V.tensor_scalar(base_e[:, :], base_e[:, :], float(P), None, ALU.mult))
            step(V.tensor_tensor(dst[:, :, :], dst[:, :, :], base_e[:, :].unsqueeze(1).broadcast_to(ge), ALU.add))
            step(V.tensor_tensor(dst[:, :, :], dst[:, :, :], hot[:, :, :], ALU.mult))
            step(V.tensor_reduce(pos_f[:, :], dst[:, :, :], AX, ALU.add))
            V.tensor_copy(pos[:, :], pos_f[:, :]).then_inc(s_pos, 1)

            first_low_parts(dve, GATE, range(CH))
            step(V.tensor_scalar(used[:, :], n_tiles[:, :], 0.0, None, ALU.is_gt))
            rank_e = sums([used, *ranks])
            ee = [P, E, E]
            step(V.tensor_scalar(last_q[:, :], iota_e[:, :], rank_e[:, E - 1:E], -1.0, ALU.subtract, ALU.is_ge))
            step(V.tensor_scalar(last_q[:, :], last_q[:, :], end_e[:, E - 1:E], None, ALU.mult))
            step(V.tensor_scalar(rank_e[:, :], rank_e[:, :], -1.0, None, ALU.add))
            step(V.tensor_tensor(match[:, :, :], rank_e[:, :].unsqueeze(1).broadcast_to(ee),
                                 iota_e[:, :].unsqueeze(2).broadcast_to(ee), ALU.is_equal))
            step(V.tensor_tensor(match[:, :, :], match[:, :, :], used[:, :].unsqueeze(1).broadcast_to(ee),
                                 ALU.mult))
            step(V.tensor_tensor(match2[:, :, :], match[:, :, :], iota_e[:, :].unsqueeze(1).broadcast_to(ee),
                                 ALU.mult))
            step(V.tensor_reduce(sel_e[:, :], match2[:, :, :], AX, ALU.add))
            step(V.tensor_tensor(match2[:, :, :], match[:, :, :], end_e[:, :].unsqueeze(1).broadcast_to(ee),
                                 ALU.mult))
            step(V.tensor_reduce(sel_end[:, :], match2[:, :, :], AX, ALU.add))
            step(V.tensor_tensor(sel_end[:, :], sel_end[:, :], last_q[:, :], ALU.max))
            te = [P, TILES, E]
            step(V.tensor_tensor(past[:, :, :], iota_t[:, :].unsqueeze(2).broadcast_to(te),
                                 sel_end[:, :].unsqueeze(1).broadcast_to(te), ALU.is_ge))
            step(V.tensor_reduce(tq_f[:, :], past[:, :, :], AX, ALU.add))
            V.tensor_copy(load_e[:, :], sel_e[0:1, :])
            V.tensor_copy(end_q[:, :], sel_end[0:1, :])
            V.tensor_copy(n_used[:, 0:1], end_e[0:1, E - 1:E])
            V.tensor_scalar(n_used[:, 1:2], end_e[0:1, E - 1:E], -1.0, None, ALU.add)
            V.tensor_copy(tile_q[:, :], tq_f[0:1, :]).then_inc(s_tab, 1)
            first_low_parts(dve, UP, range(CH - 1))

        def routing_scatter(eng):
            nc.gpsimd.iota(places[:, :], pattern=[[1, P]], base=1, channel_multiplier=0,
                           allow_small_or_imprecise_dtypes=True).then_inc(s_places, 1)
            eng.wait_ge(s_pos, 1)
            for g in range(G):
                nc.gpsimd.indirect_dma_start(
                    out=sorted_x[:, :], out_offset=bass.IndirectOffsetOnAxis(ap=pos[:, g:g + 1], axis=0),
                    in_=xn_all[:, g, :], in_offset=None).then_inc(s_scat[g], 16)
            for g in range(G):
                eng.wait_ge(s_scat[g], 16)
            nc.gpsimd.tensor_copy(mark_pool[:, 0:1], ones[:, 0:1]).then_inc(s_sorted, 1)
            eng.wait_ge(s_sorted, 1)

        gate_bank = pairs[0]
        up_bank = pairs[1]
        x_bank, out_bank = psum[0], psum[1]
        h_bank = psum[2:4]
        s_xs = sem("s_xs")
        s_id0 = sem("s_id0")
        s_xtr = sem("s_xtr")
        s_xT = sem("s_xT")
        s_xlo = sem("s_xlo")
        s_gate = sem("s_gate")
        s_up = sem("s_up")
        s_down = sem("s_down")
        s_silu = sem("s_silu")
        s_upc = sem("s_upc")
        s_hid = sem("s_hid")
        s_htr = sem("s_htr")
        s_hT = sem("s_hT")
        s_hlo = sem("s_hlo")
        s_ys = sem("s_ys")
        s_next = sem("s_next")
        s_held = sem("s_held")
        s_ids = sem("s_ids")
        s_clean = sem("s_clean")
        s_x2s = sem("s_x2s")
        s_add = sem("s_add_y")
        s_out = sem("s_out")

        FIRST = 5

        def tiles(eng, body):
            eng.wait_ge(s_tab, 1)
            in_use = eng.value_load(n_used[0:1, 0:1], min_val=G, max_val=TILES)
            last = eng.value_load(n_used[0:1, 1:2], min_val=G - 1, max_val=TILES - 1)
            body(0)
            with eng.Fori(1, TILES) as t:
                with eng.If(t < in_use):
                    body(t)
            return last

        def flat(t):
            return t[:, :, :].rearrange("p b t -> p (b t)")

        with nc.Block() as block:

            @block.sync
            def _(eng):
                def expert(q):
                    return eng.value_load(load_e[0:1, blk(q)], min_val=0, max_val=E - 1)

                routing_loads(eng)
                eng.wait_ge(s_tab, 1)
                second_e = expert(1)
                load_matrix(eng, GATE, second_e, DOWN, 0)
                load_matrix(eng, UP, second_e, GATE, 1)

                def load_three(q, before, q_before):
                    ahead = expert(q + 2)
                    load_matrix(eng, GATE, ahead, before, q_before)
                    load_matrix(eng, UP, ahead, GATE, q + 2)
                    load_matrix(eng, DOWN, expert(q + 1), UP, q + 2)

                load_three(0, UP, 1)
                with eng.Fori(1, E - 2) as q:
                    load_three(q, DOWN, q)
                load_matrix(eng, DOWN, expert(E - 1), DOWN, E - 2)

            @block.vector
            def _(dve):
                def split_matrix(kind, slot, count):
                    for c in range(CH):
                        hi, lo = slot_parts(kind, slot, c)
                        dve.wait_ge(s_wraw[c], (count + 1) * 16)
                        nc.vector.tensor_copy(hi, raw[:, c, :]).then_inc(s_whi, 1)
                        dve.wait_ge(s_whi, count * CH + (c + 1))
                        nc.vector.tensor_tensor(lo, raw[:, c, :], hi.bitcast(f32), ALU.subtract)\
                            .then_inc(s_ready[kind], 1)

                routing(dve)
                dve.wait_ge(s_xT, 1)
                nc.vector.tensor_tensor(flat(xT_lo), xT_raw[:, :], flat(xT_hi).bitcast(f32), ALU.subtract)\
                    .then_inc(s_xlo, 1)
                first_low_parts(dve, UP, range(CH - 1, CH))
                split_matrix(DOWN, 0, 2)
                dve.wait_ge(s_tab, 1)
                dve.wait_ge(s_sorted, 1)
                split_matrix(GATE, 1, 3)
                split_matrix(UP, 1, 4)
                with dve.Fori(0, E // 2 - 1) as pair:
                    for u in range(2):
                        q = 2 * pair + u
                        end = dve.value_load(end_q[0:1, blk(q)], min_val=1, max_val=TILES)
                        dve.wait_ge(s_gate, end)
                        split_matrix(GATE, u, 3 * q + FIRST)
                        dve.wait_ge(s_up, end)
                        split_matrix(UP, u, 3 * q + (FIRST + 1))
                        dve.wait_ge(s_down, end)
                        split_matrix(DOWN, 0, 3 * q + (FIRST + 2))
                end = dve.value_load(end_q[0:1, E - 2:E - 1], min_val=1, max_val=TILES)
                dve.wait_ge(s_down, end)
                split_matrix(DOWN, 0, 3 * E - 1)

            @block.scalar
            def _(act):
                def load(t):
                    act.dma_start(xs[:, :], sorted_x[blk(t, P), :]).then_inc(s_xs, 16)

                def x_parts(t):
                    act.wait_ge(s_xtr, t + 1)
                    nc.scalar.activation(flat(xT_hi), x_bank[:, :], ACT.Copy)
                    wait(act, s_xlo, t)
                    nc.scalar.activation(xT_raw[:, :], x_bank[:, :], ACT.Copy).then_inc(s_xT, 1)

                def out_tile(t):
                    act.wait_ge(s_down, t + 1)
                    wait(act, s_out, 16 * t)
                    nc.scalar.activation(ys[:, :], out_bank[:, :], ACT.Copy, scale=tanh_f[:, 0:1]).then_inc(s_ys, 1)

                def tile(t):
                    act.wait_ge(s_gate, t + 1)
                    nc.scalar.activation(hid[:, :], gate_bank[:, :], ACT.Silu).then_inc(s_silu, 1)
                    act.wait_ge(s_up, t + 1)
                    wait(act, s_hlo, t)
                    nc.scalar.activation(mid[:, :], up_bank[:, :], ACT.Copy).then_inc(s_upc, 1)
                    x_parts(t + 1)
                    if known(t, lambda t: t > 0):
                        out_tile(t - 1)
                    act.wait_ge(s_next, t + 2)
                    load(t + 2)
                    act.wait_ge(s_htr, t + 1)
                    act.wait_ge(s_hid, t + 1)
                    for n in range(2):
                        nc.scalar.activation(hT_hi[:, n * LB:(n + 1) * LB, :].rearrange("p b t -> p (b t)"),
                                             h_bank[n][:, :], ACT.Copy)
                    for n in range(2):
                        last = nc.scalar.activation(mid[:, n * 512:(n + 1) * 512], h_bank[n][:, :], ACT.Copy)
                    last.then_inc(s_hT, 1)

                first_high_parts(act, GATE, range(CH))
                nc.scalar.activation(mark_act[:, :], ones[:, 0:1], ACT.Silu)
                first_high_parts(act, UP, range(CH - 1))
                x_parts(0)
                first_high_parts(act, UP, range(CH - 1, CH))
                act.wait_ge(s_sorted, 1)
                load(1)
                act.dma_start(id_next[:, :], sorted_x[0:P, L - 1:L + 1]).then_inc(s_id0, 16)
                last_tile = tiles(act, tile)
                act.wait_ge(s_xs, 16 * last_tile + 32)
                out_tile(last_tile)

            @block.gpsimd
            def _(eng):
                one = ones[:, 0:1]

                def after(place, *waits):
                    for s, value in waits:
                        wait(eng, s, value)
                    nc.gpsimd.tensor_tensor(mark_pool[:, place:place + 1], one, one, ALU.mult)

                def low_x(t):
                    eng.wait_ge(s_xT, t + 1)
                    nc.gpsimd.tensor_tensor(flat(xT_lo), xT_raw[:, :], flat(xT_hi).bitcast(f32), ALU.subtract)\
                        .then_inc(s_xlo, 1)
                    keep_numbers(t)

                def keep_numbers(t):
                    wait(eng, s_held, t)
                    nc.gpsimd.tensor_tensor(id_next[:, 1:2], xs[:, L:L + 1], one, ALU.mult).then_inc(s_next, 1)

                def out_rows(t):
                    eng.wait_ge(s_ys, t + 1)
                    eng.wait_ge(s_x2s, 16 * (t + 1))
                    nc.gpsimd.tensor_tensor(ys[:, :], ys[:, :], x2s[:, :], ALU.add).then_inc(s_add, 1)
                    after(0, (s_add, t + 1))
                    nc.gpsimd.indirect_dma_start(
                        out=out.rearrange("g p n -> (g p) n"),
                        out_offset=bass.IndirectOffsetOnAxis(ap=id_rows[:, 0:1], axis=0),
                        in_=ys[:, :], in_offset=None, bounds_check=G * P - 1, oob_is_err=False).then_inc(s_out, 16)

                def hold_numbers(t):
                    eng.wait_ge(s_next, t + 1)
                    nc.gpsimd.tensor_tensor(id_held[:, :], id_next[:, 1:2], one, ALU.mult).then_inc(s_held, 1)

                def tile(t):
                    first = isinstance(t, int)
                    if not first:
                        hold_numbers(t)
                    eng.wait_ge(s_silu, t + 1)
                    eng.wait_ge(s_upc, t + 1)
                    nc.gpsimd.tensor_tensor(hid[:, :], hid[:, :], mid[:, :], ALU.mult).then_inc(s_hid, 1)
                    if first:
                        eng.wait_ge(s_id0, 16)
                        nc.gpsimd.tensor_tensor(mark_pool[:, 1:2], one, one, ALU.mult).then_inc(s_next, 1)
                        hold_numbers(t)
                    low_x(t + 1)
                    if known(t, lambda t: t > 0):
                        out_rows(t - 1)
                    eng.wait_ge(s_hT, t + 1)
                    nc.gpsimd.tensor_tensor(flat(hT_lo), mid[:, :], flat(hT_hi).bitcast(f32), ALU.subtract)\
                        .then_inc(s_hlo, 1)
                    after(1, (s_held, t + 1), (s_out, 16 * t))
                    nc.gpsimd.tensor_copy(id_rows[:, :], id_held[:, :]).then_inc(s_ids, 1)
                    after(2, (s_ids, t + 1))
                    nc.gpsimd.indirect_dma_start(
                        out=x2s[:, :], out_offset=None, in_=x2_dram[:, :, :].rearrange("g p n -> (g p) n"),
                        in_offset=bass.IndirectOffsetOnAxis(ap=id_rows[:, 0:1], axis=0),
                        bounds_check=G * P - 1, oob_is_err=False).then_inc(s_x2s, 16)

                routing_scatter(eng)
                nc.gpsimd.memset(x2s[:, :], 0.0).then_inc(s_clean, 1)
                eng.wait_ge(s_clean, 1)
                last_tile = tiles(eng, tile)
                out_rows(last_tile)
                eng.wait_ge(s_out, 16 * (last_tile + 1))

            @block.tensor
            def _(pe):
                def expert_of(t):
                    return pe.value_load(tile_q[0:1, blk(t)], min_val=0, max_val=E - 1)

                def x_in_array(t):
                    pe.wait_ge(s_xs, 16 * t)
                    wait(pe, s_xT, t)
                    for b in range(LB):
                        last = nc.tensor.transpose(x_bank[:, b * P:(b + 1) * P], xs[:, b * P:(b + 1) * P],
                                                   ident[:, :])
                    last.then_inc(s_xtr, 1)

                def project(bank, weights, slot, done):
                    for half in range(I // 512):
                        for b in range(LB):
                            hi = slot * (2 * MW) + (b * I + half * 512)
                            lo = slot * (2 * MW) + (MW + b * I + half * 512)
                            for n, (a, o) in enumerate(((xT_hi, hi), (xT_hi, lo), (xT_lo, hi))):
                                last = nc.tensor.matmul(bank[:, half * 512:(half + 1) * 512], a[:, b, :],
                                                        weights[:, bass.ds(o, 512)],
                                                        start=(b == 0 and n == 0), stop=(b == LB - 1 and n == 2))
                    last.then_inc(done, 1)

                def down(t):
                    q = expert_of(t)
                    pe.wait_ge(s_hlo, t + 1)
                    wait(pe, s_ys, t)
                    for b in range(IB):
                        if b % 2 == 0:
                            pe.wait_ge(s_ready[DOWN], q * CH + (b // 2 + 1))
                        for n, (a, w) in enumerate(((hT_hi, down_hi), (hT_hi, down_lo), (hT_lo, down_hi))):
                            last = nc.tensor.matmul(out_bank[:, :], a[:, b, :], w[:, b * 512:(b + 1) * 512],
                                                    start=(b == 0 and n == 0), stop=(b == IB - 1 and n == 2))
                    last.then_inc(s_down, 1)

                def tile(t):
                    q = expert_of(t)
                    slot = q % 2
                    pe.wait_ge(s_xlo, t + 1)
                    wait(pe, s_silu, t)
                    pe.wait_ge(s_ready[GATE], (q + 1) * CH)
                    project(gate_bank, gate, slot, s_gate)
                    wait(pe, s_upc, t)
                    pe.wait_ge(s_ready[UP], (q + 1) * CH)
                    project(up_bank, up, slot, s_up)
                    x_in_array(t + 1)
                    if known(t, lambda t: t > 0):
                        down(t - 1)
                    pe.wait_ge(s_hid, t + 1)
                    wait(pe, s_hT, t)
                    for b in range(IB):
                        last = nc.tensor.transpose(h_bank[b // LB][:, (b % LB) * P:(b % LB + 1) * P],
                                                   hid[:, b * P:(b + 1) * P], ident[:, :])
                    last.then_inc(s_htr, 1)

                routing_counts(pe)
                for b in range(LB):
                    for g in range(G):
                        if b == 0:
                            pe.wait_ge(s_sel, g + 1)
                        last = nc.tensor.matmul(x_bank[:, b * P:(b + 1) * P], xn_all[:, g, b * P:(b + 1) * P],
                                                select[:, g, :], start=(g == 0), stop=(g == G - 1))
                last.then_inc(s_xtr, 1)
                last_tile = tiles(pe, tile)
                down(last_tile)


_NAMES = {
    "x_rows": "x", "ctx_cols": "ctx_2048", "skip": "fside_S2_0", "g_xattn": "g_xattn", "g_ffn": "g_ffn",
    "k": "L0_xattn_k", "router_w": "L0_ffn_router_w", "gate_w": "L0_ffn_gate_w", "up_w": "L0_ffn_up_w",
    "down_w": "L0_ffn_down_w",
}


def kernel(**inputs):
    import numpy as np
    import concourse.bacc as bacc
    from concourse import mybir as mb
    from concourse.bass_utils import run_bass_kernel_spmd

    nb, d, length = inputs["x"].shape
    groups = d // 16

    def by_group(a):
        a = np.asarray(a).reshape(nb, groups, 16, length).transpose(1, 0, 2, 3)
        return a.reshape(groups, nb * 16, length)

    arrays = {n: np.asarray(inputs[m]) for n, m in _NAMES.items()}
    arrays["x_rows"] = by_group(inputs["x"])
    cols = by_group(inputs["ctx_2048"]).reshape(groups, nb * 16, length // 128, 128)
    arrays["ctx_cols"] = cols.transpose(0, 3, 2, 1).reshape(groups, 128, length // 128 * nb * 16)
    nc = bacc.Bacc("TRN2", target_bir_lowering=False, num_devices=1)
    args = []
    for name, a in arrays.items():
        arrays[name] = a = np.ascontiguousarray(a)
        args.append(nc.dram_tensor(name, a.shape, mb.dt.from_np(a.dtype), kind="ExternalInput").ap())
    args.append(nc.dram_tensor("out", arrays["x_rows"].shape, mb.dt.float32, kind="ExternalOutput").ap())
    flamingo_layer_kernel(nc, *args)
    got = run_bass_kernel_spmd(nc, [arrays], core_ids=[0]).results[0]["out"]
    return got.reshape(groups, nb, 16, length).transpose(1, 0, 2, 3).reshape(nb, d, length)
```
